# Optimizing a Trainium2 kernel written in Bass

```python
import numpy as np
import jax
import jax.numpy as jnp

def _softmax(x, axis=-1):
    return jax.nn.softmax(x, axis=axis)

def _gelu(x):
    return jax.nn.gelu(x, approximate=True)

def _silu(x):
    return jax.nn.silu(x)

def _sigmoid(x):
    return jax.nn.sigmoid(x)

def _layernorm(x, axis=-1, eps=1e-05):
    m = jnp.mean(x, axis=axis, keepdims=True)
    v = jnp.var(x, axis=axis, keepdims=True)
    return (x - m) / jnp.sqrt(v + eps)

def _scatter_add(tgt, idx, src, axis=0):
    return tgt.at[idx].add(src)

def _segment_sum(src, seg, n):
    return jax.ops.segment_sum(src, seg, n)
kernel_name = 'mk_xattn_ffn_d1_seqx_r2_276421'

def setup_inputs(seed: int=0):
    np.random.seed(seed)
    _w = jnp.asarray

    def _rec_inputs():
        import jax
        import jax.numpy as jnp
        _rk = jax.random.key(seed)
        x = -0.0002928 + 1 * jax.random.normal(jax.random.fold_in(_rk, 1), (8, 1024, 512), jnp.float32)
        _lenS = 1024 - jax.random.randint(jax.random.fold_in(_rk, 7), (8,), 0, max(1, 1024 // 4) + 1, jnp.int32)
        _lenS2 = 1024 - jax.random.randint(jax.random.fold_in(_rk, 8), (8,), 0, max(1, 1024 // 4) + 1, jnp.int32)
        _ctx_1024P = jax.random.normal(jax.random.fold_in(_rk, 11), (8, 16, 512), jnp.float32)
        _ctx_1024c = jax.random.dirichlet(jax.random.fold_in(_rk, 511), 0.3 * jnp.ones((16,), jnp.float32), (8, 1024))
        _ctx_1024t = jnp.einsum('bsk,bkd->bsd', _ctx_1024c, _ctx_1024P)
        _ctx_1024t = _ctx_1024t * jax.lax.rsqrt(jnp.mean(jnp.square(_ctx_1024t)) + 1e-12) * 0.953939
        ctx_1024 = -1.39393e-06 + 0.999914 * (_ctx_1024t + 0.3 * jax.random.normal(jax.random.fold_in(_rk, 611), (8, 1024, 512), jnp.float32))
        return (x, ctx_1024)
    x, ctx_1024 = _rec_inputs()

    def _L0_xattn_setup():
        import jax, jax.numpy as jnp
        import numpy as np
        D_MODEL = 512
        N_HEADS = 16
        D_K = D_MODEL // N_HEADS
        WINDOW = 128
        NEG = -1000000000.0
        key = jax.random.key(seed)
        ks = jax.random.split(key, 11)
        B, S = (2, 1024)
        scale = 1.0 / np.sqrt(D_MODEL)
        inp = {'Q': jax.random.normal(ks[0], (B, S, D_MODEL), jnp.float32), 'K': jax.random.normal(ks[1], (B, S, D_MODEL), jnp.float32), 'V': jax.random.normal(ks[2], (B, S, D_MODEL), jnp.float32), 'Wq': jax.random.normal(ks[3], (D_MODEL, D_MODEL), jnp.float32) * scale, 'bq': jnp.zeros((D_MODEL,), jnp.float32), 'Wk': jax.random.normal(ks[4], (D_MODEL, D_MODEL), jnp.float32) * scale, 'bk': jnp.zeros((D_MODEL,), jnp.float32), 'Wv': jax.random.normal(ks[5], (D_MODEL, D_MODEL), jnp.float32) * scale, 'bv': jnp.zeros((D_MODEL,), jnp.float32), 'Wo': jax.random.normal(ks[6], (D_MODEL, D_MODEL), jnp.float32) * scale, 'bo': jnp.zeros((D_MODEL,), jnp.float32)}
        return inp
    _L0_xattn_all = _L0_xattn_setup()
    _L0_xattn_in = {k: v for k, v in _L0_xattn_all.items() if k in ('Wq', 'bq', 'Wk', 'bk', 'Wv', 'bv', 'Wo', 'bo')}
    del _L0_xattn_all

    def _L0_ffn_setup():
        import jax, jax.numpy as jnp
        import numpy as np
        DMODEL = 512
        N_EXPERTS = 16
        EXPERT_SIZE = 128
        K = 4
        key = jax.random.key(seed)
        k1, k2, k3, k4 = jax.random.split(key, 4)
        std_sel = 1.0 / np.sqrt(DMODEL)
        std_val = 1.0 / np.sqrt(N_EXPERTS * EXPERT_SIZE)
        return {'x': jax.random.normal(k1, (4, 1024, DMODEL), dtype=jnp.float32), 'expert_sel': jax.random.normal(k2, (N_EXPERTS, DMODEL), dtype=jnp.float32) * std_sel, 'keys': jax.random.normal(k3, (N_EXPERTS, DMODEL, EXPERT_SIZE), dtype=jnp.float32) * std_sel, 'values': jax.random.normal(k4, (N_EXPERTS, EXPERT_SIZE, DMODEL), dtype=jnp.float32) * std_val, 'route_scale': jnp.ones((1,), dtype=jnp.float32)}
    _L0_ffn_all = _L0_ffn_setup()
    _L0_ffn_in = {k: v for k, v in _L0_ffn_all.items() if k in ('expert_sel', 'keys', 'values', 'route_scale')}
    del _L0_ffn_all
    return {'x': x, 'ctx_1024': ctx_1024, 'L0_xattn_Wq': _L0_xattn_in['Wq'], 'L0_xattn_bq': _L0_xattn_in['bq'], 'L0_xattn_Wk': _L0_xattn_in['Wk'], 'L0_xattn_bk': _L0_xattn_in['bk'], 'L0_xattn_Wv': _L0_xattn_in['Wv'], 'L0_xattn_bv': _L0_xattn_in['bv'], 'L0_xattn_Wo': _L0_xattn_in['Wo'], 'L0_xattn_bo': _L0_xattn_in['bo'], 'L0_ffn_expert_sel': _L0_ffn_in['expert_sel'], 'L0_ffn_keys': _L0_ffn_in['keys'], 'L0_ffn_values': _L0_ffn_in['values'], 'L0_ffn_route_scale': _L0_ffn_in['route_scale']}

def reference(x, ctx_1024, L0_xattn_Wq, L0_xattn_bq, L0_xattn_Wk, L0_xattn_bk, L0_xattn_Wv, L0_xattn_bv, L0_xattn_Wo, L0_xattn_bo, L0_ffn_expert_sel, L0_ffn_keys, L0_ffn_values, L0_ffn_route_scale):
    import jax
    import jax.numpy as jnp

    def _L0_xattn_ref(Q, K, V, Wq, bq, Wk, bk, Wv, bv, Wo, bo):
        import jax, jax.numpy as jnp
        import numpy as np
        D_MODEL = 512
        N_HEADS = 16
        D_K = D_MODEL // N_HEADS
        WINDOW = 128
        NEG = -1000000000.0
        B, S, _ = Q.shape
        q = Q @ Wq + bq
        k = K @ Wk + bk
        v = V @ Wv + bv
        q = q.reshape(B, S, N_HEADS, D_K).transpose(0, 2, 1, 3)
        k = k.reshape(B, S, N_HEADS, D_K).transpose(0, 2, 1, 3)
        v = v.reshape(B, S, N_HEADS, D_K).transpose(0, 2, 1, 3)
        scores = jnp.einsum('bhqd,bhkd->bhqk', q, k) / jnp.sqrt(jnp.float32(D_K))
        rel = jnp.arange(S)[None, :] - jnp.arange(S)[:, None]
        win = (rel >= -WINDOW) & (rel <= WINDOW)
        scores = jnp.where(win[None, None], scores, NEG)
        probs = jax.nn.softmax(scores, axis=-1)
        out = jnp.einsum('bhqk,bhkd->bhqd', probs, v)
        out = out.transpose(0, 2, 1, 3).reshape(B, S, D_MODEL)
        return out @ Wo + bo

    def _L0_ffn_ref(x, expert_sel, keys, values, route_scale):
        import jax, jax.numpy as jnp
        import numpy as np
        DMODEL = 512
        N_EXPERTS = 16
        EXPERT_SIZE = 128
        K = 4
        sel_logits = jnp.einsum('btd,ed->bte', x, expert_sel)
        sel_probs = jax.nn.sigmoid(sel_logits)
        _, sel_index = jax.lax.top_k(sel_probs, K)
        sel_val = jnp.take_along_axis(sel_probs, sel_index, axis=-1)
        sel_val = sel_val / jnp.clip(sel_val.sum(-1, keepdims=True), 1e-09)
        sel_val = sel_val * route_scale
        scores_all = jax.nn.relu(jnp.einsum('btd,edh->bteh', x, keys))
        values_all = jnp.einsum('bteh,ehv->btev', scores_all, values)
        sel_idx_exp = sel_index[..., None]
        selected = jnp.take_along_axis(values_all, sel_idx_exp, axis=2)
        out = (selected * sel_val[..., None]).sum(axis=2)
        return out
    x = x + _L0_xattn_ref(_layernorm(x, axis=-1), ctx_1024, ctx_1024, L0_xattn_Wq, L0_xattn_bq, L0_xattn_Wk, L0_xattn_bk, L0_xattn_Wv, L0_xattn_bv, L0_xattn_Wo, L0_xattn_bo)
    x = x + _L0_ffn_ref(_layernorm(x, axis=-1), L0_ffn_expert_sel, L0_ffn_keys, L0_ffn_values, L0_ffn_route_scale)
    return x

_drawn_inputs = setup_inputs


def setup_inputs(seed=0):
    import zlib

    import numpy as np

    out = dict(_drawn_inputs(seed))
    spreads = {'L0_xattn_bq': (0.0, 0.361),
     'L0_xattn_bk': (0.0, 0.8),
     'L0_xattn_bv': (0.0, 0.1),
     'L0_xattn_bo': (0.0, 0.1)}
    factors = {}
    for name, (base, spread) in spreads.items():
        noise = np.random.default_rng([zlib.crc32(name.encode()), seed]).standard_normal(out[name].shape)
        drawn = base * np.exp(spread * noise) if base else spread * noise
        out[name] = jnp.asarray(drawn.astype(out[name].dtype))
    for name, factor in factors.items():
        out[name] = (out[name] * factor).astype(out[name].dtype)
    return out
```

```python
from contextlib import ExitStack

import concourse.bass as bass
from concourse import mybir

ALU = mybir.AluOpType
ACT = mybir.ActivationFunctionType
F32 = mybir.dt.float32
F32R = mybir.dt.float32r
BF16 = mybir.dt.bfloat16
AX_X = mybir.AxisListType.X

P = 128
B, SEQ, D = 8, 1024, 512
HEADS, DK = 16, 32
C = D // P
NT = SEQ // P
HG = P // DK
UNITS = C * NT * HG
HALF = SEQ // 2
NE, TOPK = 16, 4
BLK = 512
NB = B * SEQ // BLK
TB = BLK // P
EPS = 1e-5
SCALE = 1.0 / float(DK) ** 0.5
MASKED = -1e30
BIG = 3e38
CREDIT = 64

LAG = 4
NP_ = 5
NSM = 3
NST = 4
STK_DMAS = 3 * HG


class Steps:

    def __init__(self, items):
        self.items = items
        self.total = {}
        self.ordinal = {}
        self.seen = {}
        for it in items:
            self.seen[it] = dict(self.total)
            self.total[it[0]] = self.total.get(it[0], 0) + 1
            self.ordinal[it] = self.total[it[0]]
        self.total["turn even"] = self.total.get("turn", 0) // 2


class Count:

    def __init__(self, steps, before):
        self.steps, self.before = steps, before

    def upto(self, item, back=0):
        return self.before(item[0]) + (CREDIT + self.steps.ordinal[item] - back)

    def ahead(self, kind, item, back=0):
        return self.before(kind) + (CREDIT + self.steps.seen[item].get(kind, 0) - back)


def ln_steps(t):
    return [("load_x", t), ("load_c", t), ("ln_stats", t), ("ln_rstd", t), ("ln_apply", t)]


def chained(jobs):
    out = []
    for n, job in enumerate(jobs):
        out += [("job", *job)]
        if n:
            out += [("evac", *jobs[n - 1])] + after_evac(jobs[n - 1])
    return out + [("evac", *jobs[-1])] + after_evac(jobs[-1])


def after_evac(job):
    if job[0] == "qk":
        return [("stack", *job[1:])]
    if job[0] == "out":
        return [("store", job[1])] + ([("load_res", job[1] + 2), ("res_bias", job[1] + 2)] if job[1] + 2 < NT else [])
    return []


def qk_jobs(g):
    return [("qk", g, x, half) for half in range(2) for x in "qk"]


def first_steps():
    items = []
    for t in range(NT):
        items += ln_steps(t) + chained([("tx", t), ("tc", t)])
    return Steps(items + chained(qk_jobs(0) + [("v", t) for t in range(NT)]))


def batch_steps(last):
    at = {}

    def put(slot, *steps):
        at.setdefault(slot, []).extend(steps)

    per_group = NT * HG
    for g in range(C - 1):
        s0 = g * per_group
        for n, job in enumerate(qk_jobs(g + 1)):
            put(s0 + 5 + 6 * n, ("job", *job))
            put(s0 + 6 + 6 * n, ("evac", *job))
            put(s0 + (20, 24, 32, 32)[n], ("stack", *job[1:]))
    if not last:
        s0 = (C - 1) * per_group
        for t in range(NT):
            put(s0 - 6 + 4 * t, ("load_x", t), ("load_c", t))
            put(s0 - 3 + 4 * t, ("ln_stats", t))
            put(s0 - 2 + 4 * t, ("ln_rstd", t))
            put(s0 - 1 + 4 * t, ("ln_apply", t))
            put(s0 + 4 * t, ("job", "tx", t))
            put(s0 + 4 * t + 1, ("evac", "tx", t))
            put(s0 + 4 * t + 2, ("job", "tc", t))
            put(s0 + 4 * t + 3, ("evac", "tc", t))
    items = []
    for s in range(UNITS + LAG + 3):
        if s < UNITS:
            items += [("score", s)]
        if 0 <= s - 1 < UNITS:
            items += [("norm", s - 1)]
        u = s - LAG
        if 0 <= u < UNITS:
            items += [("turn", u)]
        u = s - LAG - 2
        if u >= 0 and u % HG == HG - 1:
            g, t = divmod(u // HG, NT)
            ks = ([t - 1] if t else []) + ([t] if t == NT - 1 else [])
            items += [("pv", g, k) for k in ks]
            if t == NT // 2 + 1:
                items += [("o_evac", g, 0)]
            if t == NT - 1:
                items += [("o_evac", g, 1)]
        items += at.pop(s, [])
    assert not at
    jobs = [("out", t) for t in range(NT)]
    if not last:
        jobs = qk_jobs(0) + jobs + [("v", t) for t in range(NT)]
    items += [("load_res", 0), ("res_bias", 0), ("load_res", 1), ("res_bias", 1)]
    return Steps(items + chained(jobs))


def prepare(par, t):
    return [("ln2_stats", par, t), ("ln2_rstd", par, t), ("ln2_apply", par, t)]


ROUTE = ("logits", "logits_evac", "logits_turn", "route", "gates_turn", "gates_evac")


def block_steps(par, last):
    at = {}
    if not last:
        for t in range(TB):
            at.setdefault(t, []).extend(prepare(1 - par, t))
            at.setdefault(t + 1, []).append(("turn2", 1 - par, t))
            at.setdefault(t + 2, []).append(("turn2_evac", 1 - par, t))
        for n, kind in enumerate(ROUTE):
            at.setdefault(TB + 2 + n, []).append((kind, 1 - par))
    items = [] if last else [("load_x2", 1 - par)]
    for e in range(NE):
        if e + 1 < NE:
            items += [("gate", par, e + 1), ("hidden", par, e + 1)]
        elif not last:
            items += [("gate", 1 - par, 0), ("hidden", 1 - par, 0)]
        items += [("value", par, e)] + at.pop(e, [])
    assert not at
    return items + [("final", par, t) for t in range(TB)]


def first_block_steps():
    items = [("load_x2", 0)]
    for t in range(TB):
        items += prepare(0, t) + [("turn2", 0, t), ("turn2_evac", 0, t)]
    return Steps(items + [(kind, 0) for kind in ROUTE] + [("gate", 0, 0), ("hidden", 0, 0)])


def build_kernel(nc, x, ctx_in, wq, bq, wk, bk, wv, bv, wo, bo, sel, keys, values, route_scale, out):
    xf = x.rearrange("b s d -> (b s) d")
    cf = ctx_in.rearrange("b s d -> (b s) d")
    outf = out.rearrange("b s d -> (b s) d")
    x2f = nc.dram_tensor("x2_scratch", (B * SEQ, D), F32, kind="Internal").ap()

    with ExitStack() as whole:
        def sem(name):
            return whole.enter_context(nc.semaphore(name))

        psum = [whole.enter_context(nc.psum_tensor(f"bank{i}", [P, 512], F32)) for i in range(8)]

        def wait_alone(eng, semaphore, value):
            eng.wait_ge(semaphore, value)
            if not isinstance(value, int) and eng.engine in waited:
                eng.sem_inc(waited[eng.engine], 1)

        def rounds_of(first, steady, final, count):
            def rounds(eng, walk):
                def before(b):
                    return lambda k: b * steady.total.get(k, 0) + first.total.get(k, 0)
                walk(first, Count(first, lambda k: 0), 0, True)
                with eng.Fori(0, count) as b:
                    walk(steady, Count(steady, before(b)), b, False)
                walk(final, Count(final, before(count)), count, False)
            return rounds

        waited = {nc.gpsimd.engine: sem("pool_waited"), nc.vector.engine: sem("dve_waited"),
                  nc.sync.engine: sem("sp_waited"), nc.tensor.engine: sem("pe_waited")}
        scores, masked, exped = sem("scores"), sem("masked"), sem("exped")
        inverted, normed = sem("inverted"), sem("normed")
        transposed, pt_by_act, pt_by_dve = sem("transposed"), sem("pt_by_act"), sem("pt_by_dve")
        pv_done, o_free = sem("pv_done"), sem("o_free")
        job_full, job_hi, job_free = sem("job_full"), sem("job_hi"), sem("job_free")
        stats_done, rstd_done, xn_ready = sem("stats_done"), sem("rstd_done"), sem("xn_ready")
        res_ready = sem("res_ready")
        stats2, rstd2, xn2 = sem("stats2"), sem("rstd2"), sem("xn2")
        turned2, x2t_hi, x2t_ready = sem("turned2"), sem("x2t_hi"), sem("x2t_ready")
        logits_done, logits_out, logits_tok = sem("logits_done"), sem("logits_out"), sem("logits_tok")
        router_exp, gates_ready, gates_turned, gates_out = (
            sem("router_exp"), sem("gates_ready"), sem("gates_turned"), sem("gates_out"))
        gate_full, gate_ready, hidden_full = sem("gate_full"), sem("gate_ready"), sem("hidden_full")
        gated, gated_hi, gated_lo, value_done = sem("gated"), sem("gated_hi"), sem("gated_lo"), sem("value_done")
        finals = sem("finals")
        got_const, got_weight = sem("got_const"), sem("got_weight")
        got_x = [sem(f"got_x{i}") for i in range(2)]
        got_c = [sem(f"got_c{i}") for i in range(2)]
        got_res = [sem(f"got_res{i}") for i in range(2)]
        stored = [sem(f"stored{i}") for i in range(2)]
        stacked = {(q, half): sem(f"stacked_{q}{half}") for q in "qk" for half in range(2)}
        got_x2 = [sem(f"got_x2_{i}") for i in range(2)]
        out_stored = [sem(f"out_stored{i}") for i in range(2)]
        credits = [scores, masked, exped, inverted, normed, transposed, pt_by_act, pt_by_dve, pv_done, o_free,
                   job_full, job_hi, job_free, stats_done, rstd_done, xn_ready, res_ready, *stored, *out_stored,
                   stats2, rstd2, xn2, turned2, x2t_hi, x2t_ready, logits_done, logits_out, logits_tok,
                   router_exp, gates_ready, gates_turned, gates_out, gate_full, gate_ready, hidden_full,
                   gated, gated_hi, gated_lo, value_done, finals]
        dve_own, dve_linked, pool_own = sem("dve_own"), sem("dve_linked"), sem("pool_own")
        split_hi, split_lo, got_stage = sem("split_hi"), sem("split_lo"), [sem(f"got_stage{i}") for i in range(2)]
        sel_turned, sel_split = sem("sel_turned"), sem("sel_split")
        ident = whole.enter_context(nc.sbuf_tensor("ident", [P, P], F32))
        ident_bf = whole.enter_context(nc.sbuf_tensor("ident_bf", [P, P], BF16))
        pick = whole.enter_context(nc.sbuf_tensor("pick", [P, NE], BF16))
        half_neg = whole.enter_context(nc.sbuf_tensor("half_neg", [P, 1], F32))
        scale_col = whole.enter_context(nc.sbuf_tensor("scale_col", [P, 1], F32))

        with ExitStack() as phase1:
            def sb(name, shape, dt=F32):
                return phase1.enter_context(nc.sbuf_tensor(name, shape, dt))

            w = {n: sb(f"w_{n}", [P, C, D]) for n in "qkvo"}
            bias = {n: sb(f"bias_{n}", [P, C]) for n in "qk"}
            bias_v, bias_o = sb("bias_v", [P, D]), sb("bias_o", [P, D])
            window = sb("window", [P, 3 * P])
            x_in, c_in, res = sb("x_in", [P, 2, D]), sb("c_in", [P, 2, D]), sb("res", [P, 2, D])
            x_norm = sb("x_norm", [P, 2, D])
            ln_st, ln_mv = sb("ln_st", [P, 2, 6]), sb("ln_mv", [P, 2, 2])
            ln_rs = sb("ln_rs", [P, 2, 1])
            x_t, c_t = sb("x_t", [P, C, SEQ]), sb("c_t", [P, C, SEQ])
            v_nat = sb("v_nat", [P, NT, D])
            o_t = sb("o_t", [P, C, SEQ])
            stage = {(q, half): sb(f"stage_{q}{half}", [P, 2, HALF], F32R) for q in "qk" for half in range(2)}
            stack = {q: sb(f"stack_{q}", [P, HG, SEQ], F32R) for q in "qk"}
            neg_scores = sb("neg_scores", [P, NSM, 3 * P])
            neg_max, row_sum, row_inv = sb("neg_max", [P, NST]), sb("row_sum", [P, NST]), sb("row_inv", [P, NST])
            probs = sb("probs", [P, NP_, 3 * P])
            probs_t = sb("probs_t", [P, NST, HG, 3 * P])
            score_bank, turn_bank, o_bank, job_bank = psum[0:2], psum[2:4], psum[4:6], psum[6:8]

            with nc.Block() as block:
                @block.sync
                def _(sp):
                    for n, src in (("q", wq), ("k", wk), ("v", wv), ("o", wo)):
                        sp.dma_start(w[n][:], src.rearrange("(c p) n -> p c n", p=P)).then_inc(got_weight, 16)
                    for n, src in (("q", bq), ("k", bk)):
                        sp.dma_start(bias[n][:], src.rearrange("(c p) -> p c", p=P),
                                     allow_slow_non_contiguous=True).then_inc(got_const, 16)
                    sp.dma_start(bias_v[:], bv.partition_broadcast(P)).then_inc(got_const, 16)
                    sp.dma_start(bias_o[:], bo.partition_broadcast(P)).then_inc(got_const, 16)
                    sp.dma_start(scale_col[:], route_scale.partition_broadcast(P)).then_inc(got_const, 16)
                    sp.wait_ge(got_weight, 64)
                    sp.wait_ge(got_const, 80)

                @block.gpsimd
                def _(pool):
                    for s in credits:
                        pool.sem_inc(s, CREDIT)
                    pool.memset(ident[:], 0.0).then_inc(pool_own, 1)
                    pool.memset(ident_bf[:], 0.0).then_inc(pool_own, 1)
                    pool.memset(pick[:], 0.0).then_inc(pool_own, 1)
                    pool.memset(window[:], 0.0).then_inc(pool_own, 1)
                    pool.memset(half_neg[:], -0.5)
                    pool.wait_ge(pool_own, 4)
                    for m in (ident, ident_bf):
                        pool.affine_select(out=m[:], in_=m[:], compare_op=ALU.not_equal, fill=1.0, base=0,
                                           pattern=[[-1, P]], channel_multiplier=1).then_inc(pool_own, 1)
                    for part in range(3):
                        pool.affine_select(out=pick[:], in_=pick[:], compare_op=ALU.not_equal, fill=1.0,
                                           base=-NE * part, pattern=[[-1, NE]],
                                           channel_multiplier=1).then_inc(pool_own, 1)
                        pool.wait_ge(pool_own, 7 + part)
                    pool.affine_select(out=window[:], in_=window[:], compare_op=ALU.is_ge, fill=MASKED, base=0,
                                       pattern=[[1, 3 * P]], channel_multiplier=-1).then_inc(pool_own, 1)
                    pool.wait_ge(pool_own, 10)
                    pool.affine_select(out=window[:], in_=window[:], compare_op=ALU.is_ge, fill=MASKED,
                                       base=2 * P, pattern=[[-1, 3 * P]],
                                       channel_multiplier=1).then_inc(pool_own, 1)
                    pool.wait_ge(pool_own, 11)

            first, steady, final = first_steps(), batch_steps(False), batch_steps(True)

            rounds = rounds_of(first, steady, final, B - 1)

            def keys_of(t):
                return (P if t == 0 else 0), (2 * P if t == NT - 1 else 3 * P)

            def unit(u):
                gt, h = divmod(u, HG)
                g, t = divmod(gt, NT)
                return g, t, h

            def job_parity(steps):
                assert steady.total["job"] % 2 == 0
                return 0 if steps is first else first.total["job"] % 2

            def move_turned(eng, u, n):
                g, t, h = unit(u)
                lo, hi = keys_of(t)
                wait_alone(eng, pv_done, n.before("pv") + (CREDIT + g * NT + t - 2))
                wait_alone(eng, transposed, n.upto(("turn", u)))
                dst = probs_t[:, t % NST, h, lo:hi]
                if u % 2 == 0:
                    eng.copy(dst, turn_bank[0][:, lo:hi]).then_inc(pt_by_act, 1)
                else:
                    eng.tensor_copy(dst, turn_bank[1][:, lo:hi]).then_inc(pt_by_dve, 1)

            def load_count(b, t, is_first):
                return (0 if is_first else 16 * (NT // 2)) + 16 * (t // 2 + 1) + b * (16 * (NT // 2))

            def qk_count(n, steps, args):
                order = [i[1:] for i in steps.items if i[0] == "evac" and i[1] == "qk"]
                return n.before("stack") + (CREDIT + order.index(args) + 1)

            with nc.Block() as block:
                @block.sync
                def _(sp):
                    def walk(steps, n, b, is_first):
                        here = b * SEQ if isinstance(b, int) else sp.snap(b * SEQ)
                        ahead = here if is_first else b * SEQ + SEQ if isinstance(b, int) else sp.snap(b * SEQ + SEQ)
                        for it in steps.items:
                            kind, args = it[0], it[1:]
                            if kind == "load_x":
                                t = args[0]
                                wait_alone(sp, xn_ready, n.upto(("ln_apply", t), 2))
                                sp.dma_start(x_in[:, t % 2, :], xf[bass.ds(ahead + t * P, P), :]).then_inc(got_x[t % 2], 16)
                            elif kind == "load_c":
                                t = args[0]
                                wait_alone(sp, job_full, n.upto(("job", "tc", t - 2)) if t >= 2 else n.before("job") + CREDIT)
                                sp.dma_start(c_in[:, t % 2, :], cf[bass.ds(ahead + t * P, P), :]).then_inc(got_c[t % 2], 16)
                            elif kind == "stack":
                                g, q, half = args
                                wait_alone(sp, job_free, n.upto(("evac", "qk", g, q, half)))
                                if not is_first:
                                    g0 = (g - 1) % C
                                    last_t = NT // 2 if half == 0 else NT - 1
                                    wait_alone(sp, scores, n.upto(("score", (g0 * NT + last_t) * HG + HG - 1)))
                                src = stage[q, half]
                                for row, part in enumerate((0, 0, 1) if q == "q" else (0, 1, 0)):
                                    for h in range(HG):
                                        sp.dma_start(
                                            stack[q][DK * row:DK * row + DK, h, half * HALF:half * HALF + HALF].bitcast(F32),
                                            src[DK * h:DK * h + DK, part, :].bitcast(F32)).then_inc(stacked[q, half], 16)
                            elif kind == "load_res":
                                t = args[0]
                                wait_alone(sp, stored[t % 2], b * (16 * (NT // 2)) + (CREDIT + 16 * (t // 2)))
                                sp.dma_start(res[:, t % 2, :], xf[bass.ds(here + t * P, P), :]).then_inc(got_res[t % 2], 16)
                            elif kind == "store":
                                t = args[0]
                                wait_alone(sp, job_free, n.upto(("evac", "out", t)))
                                sp.dma_start(x2f[bass.ds(here + t * P, P), :], res[:, t % 2, :]).then_inc(stored[t % 2], 16)

                    rounds(sp, walk)
                    for s in stored:
                        sp.wait_ge(s, CREDIT + 16 * (NT // 2) * B)

                @block.gpsimd
                def _(pool):
                    def walk(steps, n, b, is_first):
                        for it in steps.items:
                            kind, args = it[0], it[1:]
                            if kind == "norm":
                                u = args[0]
                                g, t, h = unit(u)
                                lo, hi = keys_of(t)
                                p = probs[:, u % NP_, lo:hi]
                                wait_alone(pool, inverted, n.upto(it))
                                pool.tensor_scalar(p, p, row_inv[:, u % NST:u % NST + 1], 1.0,
                                                   ALU.mult, ALU.mult).then_inc(normed, 1)
                            elif kind == "ln_rstd":
                                t = args[0]
                                wait_alone(pool, stats_done, n.upto(("ln_stats", t)))
                                pool.tensor_tensor(ln_rs[:, t % 2, :], ln_mv[:, t % 2, 1:2], half_neg[:],
                                                   ALU.pow).then_inc(rstd_done, 1)
                            elif kind == "res_bias":
                                t = args[0]
                                wait_alone(pool, got_res[t % 2], 16 * (t // 2 + 1) + b * (16 * (NT // 2)))
                                pool.tensor_tensor(res[:, t % 2, :], res[:, t % 2, :], bias_o[:],
                                                   ALU.add).then_inc(res_ready, 1)

                    rounds(pool, walk)

                @block.scalar
                def _(act):
                    def walk(steps, n, b, is_first):
                        for it in steps.items:
                            kind, args = it[0], it[1:]
                            if kind == "score":
                                u = args[0]
                                g, t, h = unit(u)
                                lo, hi = keys_of(t)
                                act.wait_ge(transposed, n.before("turn") + (CREDIT + u + 1 - NP_))
                                act.wait_ge(inverted, n.before("norm") + (CREDIT + u + 1 - NST))
                                act.wait_ge(masked, n.upto(it))
                                act.activation(probs[:, u % NP_, lo:hi], neg_scores[:, u % NSM, lo:hi], ACT.Exp,
                                               bias=neg_max[:, u % NST:u % NST + 1], scale=-1.0,
                                               accum_out=row_sum[:, u % NST:u % NST + 1]).then_inc(exped, 1)
                            elif kind == "turn" and args[0] % 2 == 0:
                                move_turned(act, args[0], n)
                            elif kind == "evac" and args[0] == "qk":
                                _, g, q, half = args
                                bank = job_bank[(n.steps.ordinal[it] + job_parity(steps)) % 2]
                                if not is_first:
                                    act.wait_ge(stacked[q, half], b * (16 * STK_DMAS * C)
                                               + 16 * STK_DMAS * (g if g else C))
                                act.wait_ge(job_full, n.upto(("job", *args)))
                                act.activation(stage[q, half][:, 0, :], bank[:], ACT.Identity,
                                               bias=bias[q][:, g:g + 1]).then_inc(job_hi, 1)

                    rounds(act, walk)

                @block.vector
                def _(dve):
                    def own_wait(instruction, b, k, before):
                        instruction.then_inc(dve_own, 1)
                        wait_alone(dve, dve_own, b * per + (before + k))

                    per = 2 * NT

                    def walk(steps, n, b, is_first):
                        k = 0
                        own_before = 0 if is_first else per
                        for it in steps.items:
                            kind, args = it[0], it[1:]
                            if kind == "score":
                                u = args[0]
                                g, t, h = unit(u)
                                lo, hi = keys_of(t)
                                wait_alone(dve, exped, n.upto(it, NSM))
                                wait_alone(dve, scores, n.upto(it))
                                dve.tensor_tensor_reduce(out=neg_scores[:, u % NSM, lo:hi],
                                                         in0=score_bank[u % 2][:, lo:hi], in1=window[:, lo:hi],
                                                         scale=-SCALE, scalar=BIG, op0=ALU.add, op1=ALU.min,
                                                         accum_out=neg_max[:, u % NST:u % NST + 1]).then_inc(masked, 1)
                            elif kind == "norm":
                                u = args[0]
                                wait_alone(dve, normed, n.upto(it, NST))
                                wait_alone(dve, exped, n.upto(("score", u)))
                                dve.reciprocal(row_inv[:, u % NST:u % NST + 1],
                                               row_sum[:, u % NST:u % NST + 1]).then_inc(inverted, 1)
                            elif kind == "turn" and args[0] % 2 == 1:
                                move_turned(dve, args[0], n)
                            elif kind == "o_evac":
                                g, half = args
                                wait_alone(dve, pv_done, n.upto(("pv", g, NT // 2 if half == 0 else NT - 1)))
                                dve.tensor_copy(o_t[:, g, half * HALF:half * HALF + HALF],
                                                o_bank[half][:]).then_inc(o_free, 1)
                            elif kind == "ln_stats":
                                t = args[0]
                                wait_alone(dve, got_x[t % 2], load_count(b, t, is_first))
                                k += 1
                                own_wait(dve.bn_stats(ln_st[:, t % 2, :], x_in[:, t % 2, :]), b, k, own_before)
                                k += 1
                                own_wait(dve.bn_aggr(ln_mv[:, t % 2, :], ln_st[:, t % 2, :]), b, k, own_before)
                                dve.tensor_scalar(ln_mv[:, t % 2, 1:2], ln_mv[:, t % 2, 1:2], EPS, None,
                                                  ALU.add).then_inc(stats_done, 1)
                            elif kind == "ln_apply":
                                t = args[0]
                                wait_alone(dve, rstd_done, n.upto(("ln_rstd", t)))
                                dve.tensor_scalar(x_norm[:, t % 2, :], x_in[:, t % 2, :], ln_mv[:, t % 2, 0:1],
                                                  ln_rs[:, t % 2, :], ALU.subtract, ALU.mult).then_inc(xn_ready, 1)
                            elif kind == "evac":
                                what = args[0]
                                bank = job_bank[(n.steps.ordinal[it] + job_parity(steps)) % 2]
                                wait_alone(dve, job_full, n.upto(("job", *args)))
                                if what in ("tx", "tc"):
                                    t = args[1]
                                    dst = x_t if what == "tx" else c_t
                                    dve.tensor_copy(dst[:, :, t * P:t * P + P],
                                                    bank[:].rearrange("p (c n) -> p c n", c=C)).then_inc(job_free, 1)
                                elif what == "qk":
                                    _, g, q, half = args
                                    wait_alone(dve, job_hi, qk_count(n, steps, args))
                                    dve.scalar_tensor_tensor(out=stage[q, half][:, 1, :], in0=bank[:],
                                                             scalar=bias[q][:, g:g + 1],
                                                             in1=stage[q, half][:, 0, :].bitcast(F32),
                                                             op0=ALU.add, op1=ALU.subtract).then_inc(job_free, 1)
                                elif what == "v":
                                    dve.tensor_tensor(v_nat[:, args[1], :], bank[:], bias_v[:],
                                                      ALU.add).then_inc(job_free, 1)
                                else:
                                    t = args[1]
                                    wait_alone(dve, res_ready, n.before("res_bias") + (CREDIT + t + 1))
                                    dve.tensor_tensor(res[:, t % 2, :], bank[:], res[:, t % 2, :],
                                                      ALU.add).then_inc(job_free, 1)

                    rounds(dve, walk)

                @block.tensor
                def _(pe):
                    def product(bank, chunks):
                        for c in range(C):
                            last = pe.matmul(bank, *chunks(c), start=(c == 0), stop=(c == C - 1))
                        return last

                    def walk(steps, n, b, is_first):
                        for it in steps.items:
                            kind, args = it[0], it[1:]
                            if kind == "score":
                                u = args[0]
                                g, t, h = unit(u)
                                lo, hi = keys_of(t)
                                if h == 0:
                                    needs = {0: ("q", "k", 0), NT // 2 - 1: ("k", 1), NT // 2: ("q", 1)}.get(t, ())
                                    for q in needs[:-1]:
                                        pe.wait_ge(stacked[q, needs[-1]],
                                                   b * (16 * STK_DMAS * C) + 16 * STK_DMAS * (g + 1))
                                pe.wait_ge(masked, n.upto(it, 2))
                                pe.matmul(score_bank[u % 2][:, lo:hi], stack["q"][0:3 * DK, h, t * P:t * P + P],
                                          stack["k"][0:3 * DK, h, (t - 1) * P + lo:(t - 1) * P + hi],
                                          start=True, stop=True).then_inc(scores, 1)
                            elif kind == "turn":
                                u = args[0]
                                g, t, h = unit(u)
                                lo, hi = keys_of(t)
                                moved = pt_by_act if u % 2 == 0 else pt_by_dve
                                pe.wait_ge(moved, moved_before(n) + (CREDIT + u // 2))
                                pe.wait_ge(normed, n.upto(("norm", u)))
                                for col in range(lo, hi, P):
                                    last = pe.transpose(turn_bank[u % 2][:, col:col + P],
                                                        probs[:, u % NP_, col:col + P], ident[:])
                                last.then_inc(transposed, 1)
                            elif kind == "pv":
                                g, k = args
                                last_u = (g * NT + min(k + 1, NT - 1)) * HG + HG - 1
                                pe.wait_ge(pt_by_act, moved_before(n) + (CREDIT + (last_u + 1) // 2))
                                pe.wait_ge(pt_by_dve, moved_before(n) + (CREDIT + (last_u + 1) // 2))
                                if k == 0 or k == NT // 2 - 1:
                                    half = 0 if k == 0 else 1
                                    pe.wait_ge(o_free, n.before("o_evac") + (CREDIT + 2 * g - 1 + half))
                                if k == 0 and g == 0:
                                    pe.wait_ge(job_free, n.before("evac") + CREDIT)
                                for half in range(2):
                                    q0 = max(k - 1, half * NT // 2)
                                    q1 = min(k + 2, (half + 1) * NT // 2)
                                    if q0 >= q1:
                                        continue
                                    begins = k == 0 or (half == 1 and k == NT // 2 - 1)
                                    for h in range(HG):
                                        pieces = probs_t[:, q0 % NST:q0 % NST + q1 - q0, h, :]
                                        first_col = (k - q0 + 1) * P
                                        moving = diagonal(pieces, first_col, q1 - q0)
                                        col = (q0 * P) % HALF
                                        out_cols = o_bank[half][DK * h:DK * h + DK, col:col + (q1 - q0) * P]
                                        last = pe.matmul(out_cols.rearrange("p (q n) -> p q n", n=P),
                                                         v_nat[:, k, (g * HG + h) * DK:(g * HG + h + 1) * DK], moving,
                                                         start=begins, stop=True, skip_group_check=True)
                                last.then_inc(pv_done, 1)
                            elif kind == "job":
                                what = args[0]
                                bank = job_bank[(n.steps.ordinal[it] + job_parity(steps)) % 2]
                                pe.wait_ge(job_free, n.before("evac") + (CREDIT + n.steps.ordinal[it] - 2))
                                if what == "tx":
                                    t = args[1]
                                    pe.wait_ge(xn_ready, n.upto(("ln_apply", t)))
                                    for c in range(C):
                                        last = pe.transpose(bank[:, c * P:c * P + P],
                                                            x_norm[:, t % 2, c * P:c * P + P], ident[:])
                                elif what == "tc":
                                    t = args[1]
                                    pe.wait_ge(got_c[t % 2], load_count(b, t, is_first))
                                    for c in range(C):
                                        last = pe.transpose(bank[:, c * P:c * P + P],
                                                            c_in[:, t % 2, c * P:c * P + P], ident[:])
                                elif what == "qk":
                                    _, g, q, half = args
                                    src = x_t if q == "q" else c_t
                                    if g == 0:
                                        pe.wait_ge(job_free, n.upto(("evac", "tc", NT - 1)))
                                    last = product(bank[:], lambda c: (w[q][:, c, g * P:g * P + P],
                                                                       src[:, c, half * HALF:half * HALF + HALF]))
                                elif what == "v":
                                    t = args[1]
                                    last = product(bank[:], lambda c: (c_t[:, c, t * P:t * P + P], w["v"][:, c, :]))
                                else:
                                    t = args[1]
                                    pe.wait_ge(o_free, n.before("o_evac") + (CREDIT + 2 * C - 1 + t // (NT // 2)))
                                    last = product(bank[:], lambda c: (o_t[:, c, t * P:t * P + P], w["o"][:, c, :]))
                                last.then_inc(job_full, 1)

                    def moved_before(n):
                        return n.before("turn even")

                    def diagonal(pieces, first_col, count):
                        ap = pieces[:, :, first_col:first_col + P]
                        if count == 1:
                            return ap
                        steps_ = [list(d) for d in ap.ap]
                        steps_[1][0] -= P
                        return bass.AP(tensor=ap.tensor, offset=ap.offset, ap=steps_)

                    rounds(pe, walk)

        with ExitStack() as phase2:
            def sb(name, shape, dt=F32):
                return phase2.enter_context(nc.sbuf_tensor(name, shape, dt))

            keys_w = [sb(f"keys_{n}", [P, NE, C, P], F32R) for n in ("hi", "lo")]
            values_w = [sb(f"values_{n}", [P, NE, D], F32R) for n in ("hi", "lo")]
            sel_w = [sb(f"sel_{n}", [P, C, P], F32R) for n in ("hi", "lo")]

            with nc.sbuf_tensor("w_stage", [P, 2, 2048], F32) as w_stage, \
                    nc.sbuf_tensor("sel_raw", [NE, D], F32) as sel_raw:
                per_load = 4
                loads = [("keys", e) for e in range(0, NE, per_load)] + [("values", e) for e in range(0, NE, per_load)]

                def target(n, part):
                    what, e = loads[n]
                    if what == "keys":
                        return keys_w[part][:, e:e + per_load].rearrange("p e c h -> p (e c h)")
                    return values_w[part][:, e:e + per_load].rearrange("p e n -> p (e n)")

                with nc.Block() as block:
                    @block.sync
                    def _(sp):
                        sp.dma_start(sel_raw[:], sel).then_inc(got_weight, 16)
                        for n, (what, e) in enumerate(loads):
                            if n >= 2:
                                sp.wait_ge(split_lo, n - 1)
                            dst = w_stage[:, n % 2, :]
                            if what == "keys":
                                src = keys[e:e + per_load].rearrange("e (c p) h -> p (e c) h", p=P)
                                dst = dst.rearrange("p (ec h) -> p ec h", h=P)
                            else:
                                src = values[e:e + per_load].rearrange("e h n -> h e n")
                                dst = dst.rearrange("p (e n) -> p e n", n=D)
                            sp.dma_start(dst, src).then_inc(got_stage[n % 2], 16)

                    @block.scalar
                    def _(act):
                        for n in range(len(loads)):
                            act.wait_ge(got_stage[n % 2], 16 * (n // 2 + 1))
                            act.copy(target(n, 0), w_stage[:, n % 2, :]).then_inc(split_hi, 1)

                    @block.vector
                    def _(dve):
                        for part in range(2):
                            dve.memset(sel_w[part][:].bitcast(F32), 0.0).then_inc(sel_split, 1)
                        dve.wait_ge(sel_split, 2)
                        dve.wait_ge(sel_turned, 1)
                        turned = psum[0][:, 0:C * NE].rearrange("p (c e) -> p c e", c=C)
                        dve.tensor_copy(sel_w[0][:, :, 0:NE], turned).then_inc(sel_split, 1)
                        dve.wait_ge(sel_split, 3)
                        dve.tensor_tensor(sel_w[1][:, :, 0:NE], turned, sel_w[0][:, :, 0:NE].bitcast(F32),
                                          ALU.subtract).then_inc(sel_split, 1)
                        for n in range(len(loads)):
                            dve.wait_ge(split_hi, n + 1)
                            dve.tensor_tensor(target(n, 1), w_stage[:, n % 2, :], target(n, 0).bitcast(F32),
                                              ALU.subtract).then_inc(split_lo, 1)

                    @block.tensor
                    def _(pe):
                        pe.wait_ge(got_weight, 80)
                        for c in range(C):
                            last = pe.transpose(psum[0][:, c * NE:c * NE + NE], sel_raw[:, c * P:c * P + P],
                                                ident[0:NE, 0:NE])
                        last.then_inc(sel_turned, 1)

            x2 = [sb(f"x2_{par}", [P, TB, D]) for par in range(2)]
            x2_norm = sb("x2_norm", [P, 2, D])
            st2, mv2, rs2 = sb("st2", [P, 2, 6]), sb("mv2", [P, 2, 2]), sb("rs2", [P, 2, 1])
            x2_t = [[sb(f"x2_t{par}_{n}", [P, C, BLK], F32R) for n in ("hi", "lo")] for par in range(2)]
            gated_f = sb("gated_f", [P, 2, BLK])
            gated_w = [sb(f"gated_{n}", [P, 2, BLK], F32R) for n in ("hi", "lo")]
            gate_sb = sb("gate_sb", [P, 2, BLK])
            gates_t = [sb(f"gates_t{par}", [P, BLK], BF16) for par in range(2)]
            logits_sb = sb("logits_sb", [NE, BLK])
            exps = sb("exps", [P, TB, NE])
            router = sb("router", [P, TB, NE + TOPK])
            rest = sb("rest", [P, TB, NE + TOPK])
            top8, taken = sb("top8", [P, TB, 8]), sb("taken", [P, TB, 8])
            row = sb("row", [P, 4, TB])
            gates = sb("gates", [P, 3, TB, NE])
            parts = sb("parts", [P, TB, 3 * NE], BF16)
            out_bank, hidden_bank, gate_bank, misc_bank = psum[0:4], psum[4:6], psum[6], psum[7]
            ROUTE_OWN = 12 + TB * 3
            first2 = first_block_steps()
            steady2 = Steps(block_steps(0, False) + block_steps(1, False))
            final2 = Steps(block_steps(0, False) + block_steps(1, True))
            rounds2 = rounds_of(first2, steady2, final2, NB // 2 - 1)
            PRODUCTS = ((0, 0), (0, 1), (1, 0))

            with nc.Block() as block:
                @block.sync
                def _(sp):
                    def walk(steps, n, b, is_first):
                        base = b * (2 * BLK) if isinstance(b, int) else sp.snap(b * (2 * BLK))
                        for it in steps.items:
                            kind, args = it[0], it[1:]
                            if kind == "load_x2":
                                par = args[0]
                                at = base if is_first else base + (BLK if par else 2 * BLK)
                                wait_alone(sp, out_stored[par], b * (16 * TB) + (CREDIT + (0 if is_first or par else 16 * TB)))
                                sp.dma_start(x2[par][:], x2f[bass.ds(at, BLK), :].rearrange("(t p) d -> p t d", p=P)
                                             ).then_inc(got_x2[par], 16)
                            elif kind == "final":
                                par, t = args
                                wait_alone(sp, finals, n.upto(it))
                                sp.dma_start(outf[bass.ds(base + (par * BLK + t * P), P), :],
                                             x2[par][:, t, :]).then_inc(out_stored[par], 16)

                    rounds2(sp, walk)
                    for s in out_stored:
                        sp.wait_ge(s, CREDIT + 16 * TB * (NB // 2))

                @block.gpsimd
                def _(pool):
                    def walk(steps, n, b, is_first):
                        for it in steps.items:
                            if it[0] == "ln2_rstd":
                                _, par, t = it
                                wait_alone(pool, stats2, n.upto(("ln2_stats", par, t)))
                                pool.tensor_tensor(rs2[:, t % 2, :], mv2[:, t % 2, 1:2], half_neg[:],
                                                   ALU.pow).then_inc(rstd2, 1)

                    rounds2(pool, walk)

                @block.scalar
                def _(act):
                    def walk(steps, n, b, is_first):
                        for it in steps.items:
                            kind, args = it[0], it[1:]
                            if kind == "gate":
                                par, e = args
                                act.wait_ge(gated, n.before("hidden") + (CREDIT + n.steps.ordinal[it] - 2))
                                act.wait_ge(gate_full, n.upto(it))
                                act.copy(gate_sb[:, e % 2, :], gate_bank[:]).then_inc(gate_ready, 1)
                            elif kind == "hidden":
                                par, e = args
                                act.wait_ge(value_done, n.ahead("value", it))
                                act.wait_ge(gated, n.upto(it))
                                act.copy(gated_w[0][:, e % 2, :], gated_f[:, e % 2, :]).then_inc(gated_hi, 1)
                            elif kind == "turn2_evac":
                                par, t = args
                                act.wait_ge(turned2, n.upto(("turn2", par, t)))
                                act.copy(x2_t[par][0][:, :, t * P:t * P + P],
                                         misc_bank[:].rearrange("p (c n) -> p c n", c=C)).then_inc(x2t_hi, 1)
                            elif kind == "route":
                                act.wait_ge(logits_tok, n.upto(("logits_turn", args[0])))
                                act.activation(exps[:].rearrange("p t e -> p (t e)"), misc_bank[:, 0:TB * NE],
                                               ACT.Exp, scale=-1.0).then_inc(router_exp, 1)

                    rounds2(act, walk)

                @block.vector
                def _(dve):
                    for m in (router, taken):
                        dve.memset(m[:], -1.0)
                    for par in range(2):
                        dve.memset(gates_t[par][:], 0.0)
                    dve.drain()

                    def walk(steps, n, b, is_first):
                        per_block = 2 * TB + ROUTE_OWN
                        before = 0 if is_first else per_block
                        k = 0

                        def link(instruction):
                            nonlocal k
                            k += 1
                            instruction.then_inc(dve_linked, 1)
                            wait_alone(dve, dve_linked, b * (2 * per_block) + (before + k))

                        for it in steps.items:
                            kind, args = it[0], it[1:]
                            if kind == "ln2_stats":
                                par, t = args
                                if t == 0:
                                    wait_alone(dve, got_x2[par], b * 16 + (16 if is_first or par else 32))
                                link(dve.bn_stats(st2[:, t % 2, :], x2[par][:, t, :]))
                                link(dve.bn_aggr(mv2[:, t % 2, :], st2[:, t % 2, :]))
                                dve.tensor_scalar(mv2[:, t % 2, 1:2], mv2[:, t % 2, 1:2], EPS, None,
                                                  ALU.add).then_inc(stats2, 1)
                            elif kind == "ln2_apply":
                                par, t = args
                                wait_alone(dve, rstd2, n.upto(("ln2_rstd", par, t)))
                                dve.tensor_scalar(x2_norm[:, t % 2, :], x2[par][:, t, :], mv2[:, t % 2, 0:1],
                                                  rs2[:, t % 2, :], ALU.subtract, ALU.mult).then_inc(xn2, 1)
                            elif kind == "turn2_evac":
                                par, t = args
                                wait_alone(dve, x2t_hi, n.upto(it))
                                dve.tensor_tensor(x2_t[par][1][:, :, t * P:t * P + P],
                                                  misc_bank[:].rearrange("p (c n) -> p c n", c=C),
                                                  x2_t[par][0][:, :, t * P:t * P + P].bitcast(F32),
                                                  ALU.subtract).then_inc(x2t_ready, 1)
                            elif kind == "logits_evac":
                                wait_alone(dve, logits_done, n.upto(("logits", args[0])))
                                dve.tensor_copy(logits_sb[:], misc_bank[0:NE, :]).then_inc(logits_out, 1)
                            elif kind == "route":
                                wait_alone(dve, router_exp, n.upto(it))
                                link(dve.tensor_scalar(exps[:], exps[:], 1.0, None, ALU.add))
                                link(dve.reciprocal(router[:, :, 0:NE], exps[:]))
                                for t in range(TB):
                                    link(dve.max(top8[:, t, :], router[:, t, 0:NE]))
                                link(dve.tensor_copy(taken[:, :, 0:TOPK], top8[:, :, 0:TOPK]))
                                for t in range(TB):
                                    link(dve.match_replace(out=rest[:, t, :], in_to_replace=taken[:, t, :],
                                                           in_values=router[:, t, :], imm_value=0.0))
                                link(dve.reduce_sum(row[:, 0, :], top8[:, :, 0:TOPK], axis=AX_X))
                                link(dve.tensor_scalar(row[:, 1, :], row[:, 0, :], 1e-9, None, ALU.max))
                                link(dve.reciprocal(row[:, 2, :], row[:, 1, :]))
                                link(dve.tensor_scalar(row[:, 3, :], row[:, 2, :], scale_col[:], None, ALU.mult))
                                link(dve.tensor_tensor(gates[:, 0], router[:, :, 0:NE], rest[:, :, 0:NE],
                                                       ALU.subtract))
                                for t in range(TB):
                                    instruction = dve.tensor_scalar(gates[:, 1, t, :], gates[:, 0, t, :],
                                                                    row[:, 3, t:t + 1], None, ALU.mult)
                                    if t < TB - 1:
                                        instruction.then_inc(dve_linked, 1)
                                        k += 1
                                link(instruction)
                                link(dve.tensor_copy(parts[:, :, 0:NE], gates[:, 1]))
                                link(dve.tensor_tensor(gates[:, 2], gates[:, 1], parts[:, :, 0:NE], ALU.subtract))
                                link(dve.tensor_copy(parts[:, :, NE:2 * NE], gates[:, 2]))
                                link(dve.tensor_tensor(gates[:, 0], gates[:, 2], parts[:, :, NE:2 * NE],
                                                       ALU.subtract))
                                dve.tensor_copy(parts[:, :, 2 * NE:3 * NE], gates[:, 0]).then_inc(gates_ready, 1)
                            elif kind == "gates_evac":
                                par = args[0]
                                wait_alone(dve, gates_turned, n.upto(("gates_turn", par)))
                                dve.tensor_copy(gates_t[par][0:3 * NE, :],
                                                misc_bank[0:3 * NE, 0:BLK // 2].bitcast(BF16)).then_inc(gates_out, 1)
                            elif kind == "hidden":
                                par, e = args
                                wait_alone(dve, gated_hi, n.upto(it, 2))
                                wait_alone(dve, gated_lo, n.upto(it, 2))
                                wait_alone(dve, gate_ready, n.upto(("gate", par, e)))
                                wait_alone(dve, hidden_full, n.upto(it))
                                dve.scalar_tensor_tensor(out=gated_f[:, e % 2, :], in0=hidden_bank[e % 2][:],
                                                         scalar=0.0, in1=gate_sb[:, e % 2, :], op0=ALU.max,
                                                         op1=ALU.mult).then_inc(gated, 1)
                                wait_alone(dve, value_done, n.ahead("value", it))
                                wait_alone(dve, gated_hi, n.upto(it))
                                dve.tensor_tensor(gated_w[1][:, e % 2, :], gated_f[:, e % 2, :],
                                                  gated_w[0][:, e % 2, :].bitcast(F32),
                                                  ALU.subtract).then_inc(gated_lo, 1)
                            elif kind == "final":
                                par, t = args
                                wait_alone(dve, value_done, n.upto(("value", par, NE - 1)))
                                dve.tensor_tensor(x2[par][:, t, :], out_bank[t][:], x2[par][:, t, :],
                                                  ALU.add).then_inc(finals, 1)

                    rounds2(dve, walk)

                @block.tensor
                def _(pe):
                    def walk(steps, n, b, is_first):
                        for it in steps.items:
                            kind, args = it[0], it[1:]
                            if kind == "gate":
                                par, e = args
                                pe.wait_ge(gate_ready, n.upto(it, 1))
                                if e == 0:
                                    pe.wait_ge(gates_out, n.upto(("gates_evac", par)))
                                pe.matmul(gate_bank[:], pick[:, e:e + 1].to_broadcast([P, P]), gates_t[par][:],
                                          start=True, stop=True).then_inc(gate_full, 1)
                            elif kind == "hidden":
                                par, e = args
                                pe.wait_ge(gated, n.upto(it, 2))
                                if e == 0:
                                    pe.wait_ge(x2t_ready, n.upto(("turn2_evac", par, TB - 1)))
                                for m, (c, a, m_x) in enumerate([(c, a, m_x) for c in range(C) for a, m_x in PRODUCTS]):
                                    last = pe.matmul(hidden_bank[e % 2][:], keys_w[a][:, e, c, :],
                                                     x2_t[par][m_x][:, c, :], start=(m == 0), stop=(m == 3 * C - 1))
                                last.then_inc(hidden_full, 1)
                            elif kind == "value":
                                par, e = args
                                pe.wait_ge(gated_hi, n.ahead("value", it) + 1)
                                pe.wait_ge(gated_lo, n.ahead("value", it) + 1)
                                for t in range(TB):
                                    if e == 0:
                                        pe.wait_ge(finals, n.ahead("final", it, TB - 1 - t))
                                    for m, (a, v) in enumerate(PRODUCTS):
                                        last = pe.matmul(out_bank[t][:], gated_w[a][:, e % 2, t * P:t * P + P],
                                                         values_w[v][:, e, :], start=(e == 0 and m == 0),
                                                         stop=(e == NE - 1 and m == 2))
                                last.then_inc(value_done, 1)
                            elif kind == "turn2":
                                par, t = args
                                pe.wait_ge(x2t_ready, n.ahead("turn2_evac", it))
                                pe.wait_ge(gates_out, n.ahead("gates_evac", it))
                                pe.wait_ge(xn2, n.upto(("ln2_apply", par, t)))
                                for c in range(C):
                                    last = pe.transpose(misc_bank[:, c * P:c * P + P],
                                                        x2_norm[:, t % 2, c * P:c * P + P], ident[:])
                                last.then_inc(turned2, 1)
                            elif kind == "logits":
                                par = args[0]
                                pe.wait_ge(x2t_ready, n.ahead("turn2_evac", it))
                                for m, (c, a, m_x) in enumerate([(c, a, m_x) for c in range(C) for a, m_x in PRODUCTS]):
                                    last = pe.matmul(misc_bank[:], sel_w[a][:, c, :], x2_t[par][m_x][:, c, :],
                                                     start=(m == 0), stop=(m == 3 * C - 1))
                                last.then_inc(logits_done, 1)
                            elif kind == "logits_turn":
                                wait_alone(pe, logits_out, n.upto(("logits_evac", args[0])))
                                for t in range(TB):
                                    last = pe.transpose(misc_bank[:, t * NE:t * NE + NE],
                                                        logits_sb[:, t * P:t * P + P], ident[0:NE, 0:NE])
                                last.then_inc(logits_tok, 1)
                            elif kind == "gates_turn":
                                wait_alone(pe, gates_ready, n.upto(("route", args[0])))
                                turned = misc_bank[0:3 * NE, 0:BLK // 2].bitcast(BF16)
                                for t in range(TB):
                                    last = pe.transpose(turned[:, t * P:t * P + P], parts[:, t, :], ident_bf[:])
                                last.then_inc(gates_turned, 1)

                    rounds2(pe, walk)


INPUTS = ["x", "ctx_1024", "L0_xattn_Wq", "L0_xattn_bq", "L0_xattn_Wk", "L0_xattn_bk", "L0_xattn_Wv", "L0_xattn_bv",
          "L0_xattn_Wo", "L0_xattn_bo", "L0_ffn_expert_sel", "L0_ffn_keys", "L0_ffn_values", "L0_ffn_route_scale"]


def kernel(**inputs):
    import numpy as np
    import concourse.bacc as bacc
    from concourse.bass_utils import run_bass_kernel_spmd

    nc = bacc.Bacc("TRN2", target_bir_lowering=False, num_devices=1)
    arrays, args = {}, []
    for name in INPUTS:
        a = np.ascontiguousarray(inputs[name])
        arrays[name + "_dram"] = a
        args.append(nc.dram_tensor(name + "_dram", a.shape, mybir.dt.from_np(a.dtype), kind="ExternalInput").ap())
    args.append(nc.dram_tensor("out_dram", (B, SEQ, D), F32, kind="ExternalOutput").ap())
    build_kernel(nc, *args)
    result = run_bass_kernel_spmd(nc, [arrays], core_ids=[0])
    return result.results[0]["out_dram"]
```

```python
from contextlib import ExitStack

import concourse.bass as bass
from concourse import mybir

ALU = mybir.AluOpType
ACT = mybir.ActivationFunctionType
F32 = mybir.dt.float32
F32R = mybir.dt.float32r
BF16 = mybir.dt.bfloat16
AX_X = mybir.AxisListType.X

P = 128
B, SEQ, D = 8, 1024, 512
HEADS, DK = 16, 32
C = D // P
NT = SEQ // P
HG = P // DK
TILES = C * NT
GROUP = NT * HG
UNITS = C * GROUP
HALF = SEQ // 2
NE, TOPK = 16, 4
BLK = 512
NB = B * SEQ // BLK
TB = BLK // P
EPS = 1e-5
SCALE = 1.0 / float(DK) ** 0.5
MASKED = -1e30
BIG = 3e38
CREDIT = 64

LAG = 6
RING = 8
NSM = 4
NQT = 4
NBANK = 8
NSTAGE = 4
PRODUCTS = ((0, 0), (0, 1), (1, 0))
LOAD_QK = 16 * 6
LOAD_IN = 16 * 2


class Steps:

    def __init__(self, items):
        self.items = items
        self.total = {}
        self.ordinal = {}
        self.seen = {}
        for it in items:
            self.seen[it] = dict(self.total)
            self.total[it[0]] = self.total.get(it[0], 0) + 1
            self.ordinal[it] = self.total[it[0]]


class Count:

    def __init__(self, steps, before):
        self.steps, self.before = steps, before

    def upto(self, item, back=0):
        return self.before(item[0]) + (CREDIT + self.steps.ordinal[item] - back)

    def ahead(self, kind, item, back=0):
        return self.before(kind) + (CREDIT + self.steps.seen[item].get(kind, 0) - back)


def leave(job):
    out = [] if job[0] == "v" else [("round", *job)]
    return out + [("evac", *job)] + ([("store", *job)] if job[0] in ("qk", "v") else [])


def project_steps(par, prepare_next, load_next):
    jobs = [("qk", par, g, q) for g in range(C) for q in "qk"] + [("v", par, t) for t in range(TB)]
    at = {}
    if prepare_next:
        for t in range(TB):
            at.setdefault(2 * t, []).extend([("ln_stats", 1 - par, t), ("ln_rstd", 1 - par, t)])
            at.setdefault(2 * t + 1, []).extend([("ln_apply", 1 - par, t), ("job", "tc", 1 - par, t)])
            at.setdefault(2 * t + 2, []).extend([("job", "tx", 1 - par, t)])
    items, waiting = [("load", par)] if load_next else [], []
    for n, job in enumerate(jobs):
        for it in at.pop(n, []) + [("job", *job)]:
            items.append(it)
            if it[0] == "job":
                for earlier in waiting:
                    items += leave(earlier)
                waiting = [it[1:]]
    assert not at
    return items + leave(waiting[0])


def first_project_steps():
    items = [("load", 0), ("load", 1)]
    for t in range(TB):
        items += [("ln_stats", 0, t), ("ln_rstd", 0, t), ("ln_apply", 0, t)]
        for what in ("tc", "tx"):
            items += [("job", what, 0, t)] + leave((what, 0, t))
    return Steps(items + [("settle",)])


def attention_steps(mine, after, ahead):
    at = {}

    def put(slot, *steps):
        at.setdefault(slot, []).extend(steps)

    def exists(n):
        return mine if n >= 0 else after

    if mine:
        if not after:
            put(-1, ("load_qk", 0), ("load_v", 0))
        for g in range(C if ahead else C - 1):
            put(g * GROUP, ("load_qk", g + 1))
            put(g * GROUP + 12, ("load_v", g + 1))
        put(UNITS - 36, ("o_move",))
    if after:
        put(0, ("load_res", 0), ("load_res", 1))
        put(5, ("res_bias", 0))
        put(9, ("res_bias", 1))
        for t in range(NT):
            s0 = 12 + 9 * t
            for third in range(3):
                put(s0 + third, ("out", t, third))
            put(s0 + 3, ("out_evac", t), ("store", t))
            if t + 2 < NT:
                put(s0 + 3, ("load_res", t + 2))
                put(s0 + 11, ("res_bias", t + 2))
    items = []
    for s in range(-1, UNITS):
        if s >= 0:
            if mine:
                items += [("score", s)]
            if s % 2 and exists(s - 3):
                items += [("invert", (s - 3) // 2), ("norm", s - 3), ("norm", s - 2)]
            if exists(s - LAG):
                items += [("turn", s - LAG)]
            u = s - LAG - 2
            if u % HG == HG - 1 and exists(u):
                tile = u // HG
                t = tile % NT
                items += [("pv", k) for k in ([tile - 1] if t else []) + ([tile] if t == NT - 1 else [])]
            u = s - LAG - 4
            if u % HG == HG - 1 and exists(u):
                g, t = divmod(u // HG, NT)
                if t in (NT // 2 + 1, NT - 1):
                    items += [("o_evac", g, 0 if t == NT // 2 + 1 else 1)]
        items += at.pop(s, [])
    assert not at
    return items


def prepare(par, t):
    return [("ln3_stats", par, t), ("ln3_rstd", par, t), ("ln3_apply", par, t)]


ROUTE = ("logits", "logits_evac", "logits_turn", "sigmoid", "choose", "weigh", "gates_turn", "gates_evac")


def block_steps(par, last):
    at = {}
    if not last:
        for t in range(TB):
            at.setdefault(t, []).extend(prepare(1 - par, t))
            at.setdefault(t + 1, []).append(("turn2", 1 - par, t))
            at.setdefault(t + 2, []).append(("turn2_evac", 1 - par, t))
        for n, kind in enumerate(ROUTE):
            at.setdefault(TB + 2 + n, []).append((kind, 1 - par))
    items = [] if last else [("load_x2", 1 - par)]
    for e in range(NE):
        if e + 1 < NE:
            items += [("gate", par, e + 1), ("hidden", par, e + 1)]
        elif not last:
            items += [("gate", 1 - par, 0), ("hidden", 1 - par, 0)]
        items += [("value", par, e)] + at.pop(e, [])
    assert not at
    return items + [("final", par, t) for t in range(TB)]


def first_block_steps():
    items = [("load_x2", 0)]
    for t in range(TB):
        items += prepare(0, t) + [("turn2", 0, t), ("turn2_evac", 0, t)]
    return Steps(items + [(kind, 0) for kind in ROUTE] + [("gate", 0, 0), ("hidden", 0, 0)])


def build_kernel(nc, x, ctx_in, wq, bq, wk, bk, wv, bv, wo, bo, sel, keys, values, route_scale, out):
    xf = x.rearrange("b s d -> (b s) d")
    cf = ctx_in.rearrange("b s d -> (b s) d")
    outf = out.rearrange("b s d -> (b s) d")
    x2f = nc.dram_tensor("x2_scratch", (B * SEQ, D), F32, kind="Internal").ap()
    qk_scratch = {q: nc.dram_tensor(f"{q}_scratch", (2, D, B * SEQ), F32, kind="Internal").ap() for q in "qk"}
    v_scratch = nc.dram_tensor("v_scratch", (B * SEQ, D), F32, kind="Internal").ap()

    with ExitStack() as whole:
        def sem(name):
            return whole.enter_context(nc.semaphore(name))

        psum = [whole.enter_context(nc.psum_tensor(f"bank{i}", [P, 512], F32)) for i in range(8)]

        def wait_alone(eng, semaphore, value):
            eng.wait_ge(semaphore, value)
            if not isinstance(value, int) and eng.engine in waited:
                eng.sem_inc(waited[eng.engine], 1)

        def rounds_of(first, steady, final, count):
            def rounds(eng, walk):
                def before(b):
                    return lambda k: b * steady.total.get(k, 0) + first.total.get(k, 0)
                walk(first, Count(first, lambda k: 0), 0, True)
                with eng.Fori(0, count) as b:
                    walk(steady, Count(steady, before(b)), b, False)
                walk(final, Count(final, before(count)), count, False)
            return rounds

        waited = {nc.gpsimd.engine: sem("pool_waited"), nc.vector.engine: sem("dve_waited"),
                  nc.sync.engine: sem("sp_waited"), nc.tensor.engine: sem("pe_waited")}
        stats_done, rstd_done, xn_ready = sem("stats_done"), sem("rstd_done"), sem("xn_ready")
        job_full, job_hi, job_free = sem("job_full"), sem("job_hi"), sem("job_free")
        scores, masked, exped = sem("scores"), sem("masked"), sem("exped")
        inverted, normed = sem("inverted"), sem("normed")
        transposed, pt_by_act, pt_by_dve = sem("transposed"), sem("pt_by_act"), sem("pt_by_dve")
        pv_done, o_hi, o_free = sem("pv_done"), sem("o_hi"), sem("o_free")
        out_full, out_free, res_ready = sem("out_full"), sem("out_free"), sem("res_ready")
        stats3, rstd3, xn3 = sem("stats3"), sem("rstd3"), sem("xn3")
        turned2, x2t_hi, x2t_ready = sem("turned2"), sem("x2t_hi"), sem("x2t_ready")
        logits_done, logits_out, logits_tok = sem("logits_done"), sem("logits_out"), sem("logits_tok")
        router_exp, gates_ready, gates_turned, gates_out = (
            sem("router_exp"), sem("gates_ready"), sem("gates_turned"), sem("gates_out"))
        gate_full, gate_ready, hidden_full = sem("gate_full"), sem("gate_ready"), sem("hidden_full")
        gated, gated_hi, gated_lo, value_done = sem("gated"), sem("gated_hi"), sem("gated_lo"), sem("value_done")
        finals = sem("finals")
        got_const, got_weight = sem("got_const"), sem("got_weight")
        got_in = [sem(f"got_in{i}") for i in range(2)]
        qk_stored = [sem(f"qk_stored{i}") for i in range(NSTAGE)]
        v_stored = [sem(f"v_stored{i}") for i in range(2)]
        got_qk = [sem(f"got_qk{i}") for i in range(2)]
        got_v = [sem(f"got_v{i}") for i in range(2)]
        o_moved = sem("o_moved")
        got_res = [sem(f"got_res{i}") for i in range(2)]
        stored = [sem(f"stored{i}") for i in range(2)]
        got_x2 = [sem(f"got_x2_{i}") for i in range(2)]
        out_stored = [sem(f"out_stored{i}") for i in range(2)]
        credits = [stats_done, rstd_done, xn_ready, job_full, job_hi, job_free, *qk_stored, *v_stored,
                   scores, masked, exped, inverted, normed, transposed, pt_by_act, pt_by_dve, pv_done, o_hi,
                   o_free, out_full, out_free, res_ready, *stored, *out_stored,
                   stats3, rstd3, xn3, turned2, x2t_hi, x2t_ready, logits_done, logits_out, logits_tok,
                   router_exp, gates_ready, gates_turned, gates_out, gate_full, gate_ready, hidden_full,
                   gated, gated_hi, gated_lo, value_done, finals]
        dve_own, dve_linked, pool_own = sem("dve_own"), sem("dve_linked"), sem("pool_own")
        weight_hi, weight_lo = sem("weight_hi"), sem("weight_lo")
        split_hi, split_lo, got_stage = sem("split_hi"), sem("split_lo"), [sem(f"got_stage{i}") for i in range(2)]
        sel_turned, sel_split = sem("sel_turned"), sem("sel_split")
        ident = whole.enter_context(nc.sbuf_tensor("ident", [P, P], F32))
        ident_bf = whole.enter_context(nc.sbuf_tensor("ident_bf", [P, P], BF16))
        pick = whole.enter_context(nc.sbuf_tensor("pick", [P, NE], BF16))
        half_neg = whole.enter_context(nc.sbuf_tensor("half_neg", [P, 1], F32))
        scale_col = whole.enter_context(nc.sbuf_tensor("scale_col", [P, 1], F32))

        with ExitStack() as attention:
            wo_w = [attention.enter_context(nc.sbuf_tensor(f"wo_{n}", [P, C, D], F32R)) for n in ("hi", "lo")]
            bias_o = attention.enter_context(nc.sbuf_tensor("bias_o", [P, D], F32))
            window = attention.enter_context(nc.sbuf_tensor("window", [P, 3 * P], F32))

            with ExitStack() as phase1:
                def sb(name, shape, dt=F32):
                    return phase1.enter_context(nc.sbuf_tensor(name, shape, dt))

                w = {n: [sb(f"w{n}_{part}", [P, C, D], F32R) for part in ("hi", "lo")] for n in "qkv"}
                w["o"] = wo_w
                bias = {n: sb(f"bias_{n}", [P, C]) for n in "qk"}
                bias_v = sb("bias_v", [P, D])

                with nc.sbuf_tensor("w_raw", [P, 4, C, D], F32) as w_raw, nc.Block() as block:
                    @block.sync
                    def _(sp):
                        for n, src in enumerate((wq, wk, wv, wo)):
                            sp.dma_start(w_raw[:, n], src.rearrange("(c p) n -> p c n", p=P)).then_inc(got_weight, 16)
                        for n, src in (("q", bq), ("k", bk)):
                            sp.dma_start(bias[n][:], src.rearrange("(c p) -> p c", p=P),
                                         allow_slow_non_contiguous=True).then_inc(got_const, 16)
                        sp.dma_start(bias_v[:], bv.partition_broadcast(P)).then_inc(got_const, 16)
                        sp.dma_start(bias_o[:], bo.partition_broadcast(P)).then_inc(got_const, 16)
                        sp.dma_start(scale_col[:], route_scale.partition_broadcast(P)).then_inc(got_const, 16)
                        sp.wait_ge(got_const, 80)

                    @block.scalar
                    def _(act):
                        act.wait_ge(got_weight, 64)
                        for n, name in enumerate("qkvo"):
                            act.copy(w[name][0][:], w_raw[:, n]).then_inc(weight_hi, 1)

                    @block.vector
                    def _(dve):
                        for n, name in enumerate("qkvo"):
                            dve.wait_ge(weight_hi, n + 1)
                            dve.tensor_tensor(w[name][1][:], w_raw[:, n], w[name][0][:].bitcast(F32), ALU.subtract)
                        dve.drain()

                    @block.gpsimd
                    def _(pool):
                        for s in credits:
                            pool.sem_inc(s, CREDIT)
                        pool.memset(ident[:], 0.0).then_inc(pool_own, 1)
                        pool.memset(ident_bf[:], 0.0).then_inc(pool_own, 1)
                        pool.memset(pick[:], 0.0).then_inc(pool_own, 1)
                        pool.memset(window[:], 0.0).then_inc(pool_own, 1)
                        pool.memset(half_neg[:], -0.5)
                        pool.wait_ge(pool_own, 4)
                        for m in (ident, ident_bf):
                            pool.affine_select(out=m[:], in_=m[:], compare_op=ALU.not_equal, fill=1.0, base=0,
                                               pattern=[[-1, P]], channel_multiplier=1).then_inc(pool_own, 1)
                        for part in range(3):
                            pool.affine_select(out=pick[:], in_=pick[:], compare_op=ALU.not_equal, fill=1.0,
                                               base=-NE * part, pattern=[[-1, NE]],
                                               channel_multiplier=1).then_inc(pool_own, 1)
                            pool.wait_ge(pool_own, 7 + part)
                        pool.affine_select(out=window[:], in_=window[:], compare_op=ALU.is_ge, fill=MASKED, base=0,
                                           pattern=[[1, 3 * P]], channel_multiplier=-1).then_inc(pool_own, 1)
                        pool.wait_ge(pool_own, 10)
                        pool.affine_select(out=window[:], in_=window[:], compare_op=ALU.is_ge, fill=MASKED,
                                           base=2 * P, pattern=[[-1, 3 * P]],
                                           channel_multiplier=1).then_inc(pool_own, 1)
                        pool.wait_ge(pool_own, 11)

                x_in = [sb(f"x_in{par}", [P, TB, D]) for par in range(2)]
                c_in = [sb(f"c_in{par}", [P, TB, D]) for par in range(2)]
                x_norm = sb("x_norm", [P, 2, D])
                ln_st, ln_mv, ln_rs = sb("ln_st", [P, 2, 6]), sb("ln_mv", [P, 2, 2]), sb("ln_rs", [P, 2, 1])
                x_t = [[sb(f"x_t{par}_{n}", [P, C, BLK], F32R) for n in ("hi", "lo")] for par in range(2)]
                c_t = [[sb(f"c_t{par}_{n}", [P, C, BLK], F32R) for n in ("hi", "lo")] for par in range(2)]
                qk_stage = sb("qk_stage", [P, NSTAGE, 2, BLK], F32R)
                v_stage = sb("v_stage", [P, 2, D])

                first1 = first_project_steps()
                steady1 = Steps(project_steps(0, True, True) + project_steps(1, True, True))
                final1 = Steps(project_steps(0, True, False) + project_steps(1, False, False))
                rounds1 = rounds_of(first1, steady1, final1, NB // 2 - 1)
                assert first1.total["job"] % NBANK == 0 and steady1.total["job"] % NBANK == 0
                evacs = [it[1:] for it in project_steps(0, True, True) if it[0] == "evac"]
                behind_turns = len(evacs) - 1 - evacs.index(("tx", 1, TB - 1))

                def job_bank(n, job):
                    return psum[(n.steps.ordinal[("job", *job)] - 1) % NBANK]

                def qk_slot(par, g, q):
                    number = (par * C + g) * 2 + "qk".index(q)
                    return number, number % NSTAGE

                with nc.Block() as block:
                    @block.sync
                    def _(sp):
                        def walk(steps, n, b, is_first):
                            base = b * (2 * BLK) if isinstance(b, int) else sp.snap(b * (2 * BLK))
                            for it in steps.items:
                                kind, args = it[0], it[1:]
                                if kind == "load":
                                    par = args[0]
                                    at = base + par * BLK + (0 if is_first else 2 * BLK)
                                    if not is_first:
                                        wait_alone(sp, xn_ready, n.ahead("ln_apply", it))
                                        wait_alone(sp, job_full, n.ahead("job", it))
                                    for dst, src in ((x_in, xf), (c_in, cf)):
                                        sp.dma_start(dst[par][:], src[bass.ds(at, BLK), :].rearrange(
                                            "(t p) d -> p t d", p=P)).then_inc(got_in[par], 16)
                                elif kind == "store" and args[0] == "qk":
                                    _, par, g, q = args
                                    _, slot = qk_slot(par, g, q)
                                    wait_alone(sp, job_free, n.upto(("evac", *args)))
                                    sp.dma_start(qk_scratch[q][:, g * P:g * P + P, bass.ds(base + par * BLK, BLK)
                                                               ].rearrange("a p n -> p a n"),
                                                 qk_stage[:, slot].bitcast(F32)).then_inc(qk_stored[slot], 16)
                                elif kind == "store":
                                    _, par, t = args
                                    wait_alone(sp, job_free, n.upto(("evac", *args)))
                                    sp.dma_start(v_scratch[bass.ds(base + (par * BLK + t * P), P), :],
                                                 v_stage[:, t % 2, :]).then_inc(v_stored[t % 2], 16)

                        rounds1(sp, walk)
                        for s in qk_stored:
                            sp.wait_ge(s, CREDIT + 16 * (2 * C // NSTAGE) * NB)
                        for s in v_stored:
                            sp.wait_ge(s, CREDIT + 16 * (TB // 2) * NB)

                    @block.gpsimd
                    def _(pool):
                        def walk(steps, n, b, is_first):
                            for it in steps.items:
                                if it[0] == "ln_rstd":
                                    _, par, t = it
                                    wait_alone(pool, stats_done, n.upto(("ln_stats", par, t)))
                                    pool.tensor_tensor(ln_rs[:, t % 2, :], ln_mv[:, t % 2, 1:2], half_neg[:],
                                                       ALU.pow).then_inc(rstd_done, 1)

                        rounds1(pool, walk)

                    @block.scalar
                    def _(act):
                        def walk(steps, n, b, is_first):
                            for it in steps.items:
                                kind, args = it[0], it[1:]
                                if kind != "round":
                                    continue
                                bank = job_bank(n, args)
                                if args[0] == "qk":
                                    _, par, g, q = args
                                    number, slot = qk_slot(par, g, q)
                                    act.wait_ge(qk_stored[slot], b * (16 * 4 * C // NSTAGE)
                                                + (CREDIT + 16 * (number // NSTAGE)))
                                    act.wait_ge(job_full, n.upto(("job", *args)))
                                    act.activation(qk_stage[:, slot, 0, :], bank[:], ACT.Identity,
                                                   bias=bias[q][:, g:g + 1]).then_inc(job_hi, 1)
                                else:
                                    what, par, t = args
                                    dst = (x_t if what == "tx" else c_t)[par][0]
                                    act.wait_ge(job_full, n.upto(("job", *args)))
                                    act.copy(dst[:, :, t * P:t * P + P],
                                             bank[:].rearrange("p (c n) -> p c n", c=C)).then_inc(job_hi, 1)

                        rounds1(act, walk)

                    @block.vector
                    def _(dve):
                        def walk(steps, n, b, is_first):
                            k = 0 if is_first else 2 * TB

                            def link(instruction):
                                nonlocal k
                                k += 1
                                instruction.then_inc(dve_own, 1)
                                wait_alone(dve, dve_own, b * (4 * TB) + k)

                            for it in steps.items:
                                kind, args = it[0], it[1:]
                                if kind == "ln_stats":
                                    par, t = args
                                    if t == 0:
                                        wait_alone(dve, got_in[par], b * LOAD_IN + (
                                            LOAD_IN if is_first or par else 2 * LOAD_IN))
                                    link(dve.bn_stats(ln_st[:, t % 2, :], x_in[par][:, t, :]))
                                    link(dve.bn_aggr(ln_mv[:, t % 2, :], ln_st[:, t % 2, :]))
                                    dve.tensor_scalar(ln_mv[:, t % 2, 1:2], ln_mv[:, t % 2, 1:2], EPS, None,
                                                      ALU.add).then_inc(stats_done, 1)
                                elif kind == "ln_apply":
                                    par, t = args
                                    wait_alone(dve, rstd_done, n.upto(("ln_rstd", par, t)))
                                    dve.tensor_scalar(x_norm[:, t % 2, :], x_in[par][:, t, :], ln_mv[:, t % 2, 0:1],
                                                      ln_rs[:, t % 2, :], ALU.subtract, ALU.mult).then_inc(xn_ready, 1)
                                elif kind == "evac" and args[0] == "qk":
                                    _, par, g, q = args
                                    _, slot = qk_slot(par, g, q)
                                    wait_alone(dve, job_hi, n.upto(("round", *args)))
                                    dve.scalar_tensor_tensor(out=qk_stage[:, slot, 1, :], in0=job_bank(n, args)[:],
                                                             scalar=bias[q][:, g:g + 1],
                                                             in1=qk_stage[:, slot, 0, :].bitcast(F32),
                                                             op0=ALU.add, op1=ALU.subtract).then_inc(job_free, 1)
                                elif kind == "evac" and args[0] == "v":
                                    _, par, t = args
                                    wait_alone(dve, v_stored[t % 2], b * (16 * TB) + (
                                        CREDIT + 16 * ((par * TB + t) // 2)))
                                    wait_alone(dve, job_full, n.upto(("job", *args)))
                                    dve.tensor_tensor(v_stage[:, t % 2, :], job_bank(n, args)[:], bias_v[:],
                                                      ALU.add).then_inc(job_free, 1)
                                elif kind == "evac":
                                    what, par, t = args
                                    hi, lo = (x_t if what == "tx" else c_t)[par]
                                    wait_alone(dve, job_hi, n.upto(("round", *args)))
                                    dve.tensor_tensor(lo[:, :, t * P:t * P + P],
                                                      job_bank(n, args)[:].rearrange("p (c n) -> p c n", c=C),
                                                      hi[:, :, t * P:t * P + P].bitcast(F32),
                                                      ALU.subtract).then_inc(job_free, 1)

                        rounds1(dve, walk)

                    @block.tensor
                    def _(pe):
                        def walk(steps, n, b, is_first):
                            for it in steps.items:
                                kind, args = it[0], it[1:]
                                if kind == "settle":
                                    pe.wait_ge(job_free, CREDIT + 2 * TB)
                                if kind != "job":
                                    continue
                                bank = job_bank(n, args)
                                pe.wait_ge(job_free, n.before("evac") + (CREDIT + n.steps.ordinal[it] - NBANK))
                                if args[0] == "tx":
                                    _, par, t = args
                                    pe.wait_ge(xn_ready, n.upto(("ln_apply", par, t)))
                                    for c in range(C):
                                        last = pe.transpose(bank[:, c * P:c * P + P],
                                                            x_norm[:, t % 2, c * P:c * P + P], ident[:])
                                elif args[0] == "tc":
                                    _, par, t = args
                                    if t == 0:
                                        pe.wait_ge(got_in[par], b * LOAD_IN + (
                                            LOAD_IN if is_first or par else 2 * LOAD_IN))
                                    for c in range(C):
                                        last = pe.transpose(bank[:, c * P:c * P + P],
                                                            c_in[par][:, t, c * P:c * P + P], ident[:])
                                elif args[0] == "qk":
                                    _, par, g, q = args
                                    src = (x_t if q == "q" else c_t)[par]
                                    if g == 0 and q == "q":
                                        pe.wait_ge(job_free, n.ahead("evac", it, behind_turns))
                                    for m, (c, a, s) in enumerate([(c, a, s) for c in range(C) for a, s in PRODUCTS]):
                                        last = pe.matmul(bank[:], w[q][a][:, c, g * P:g * P + P], src[s][:, c, :],
                                                         start=(m == 0), stop=(m == 3 * C - 1))
                                else:
                                    _, par, t = args
                                    for m, (c, s, a) in enumerate([(c, s, a) for c in range(C) for s, a in PRODUCTS]):
                                        last = pe.matmul(bank[:], c_t[par][s][:, c, t * P:t * P + P],
                                                         w["v"][a][:, c, :], start=(m == 0), stop=(m == 3 * C - 1))
                                last.then_inc(job_full, 1)

                        rounds1(pe, walk)

            with ExitStack() as phase2:
                def sb(name, shape, dt=F32):
                    return phase2.enter_context(nc.sbuf_tensor(name, shape, dt))

                stack = {q: [sb(f"stack_{q}{i}", [P, HG, SEQ], F32R) for i in range(2)] for q in "qk"}
                v_group = [sb(f"v_group{i}", [P, NT, P]) for i in range(2)]
                neg_scores = sb("neg_scores", [P, NSM, 3 * P])
                neg_max, row_sum, row_inv = sb("neg_max", [P, RING]), sb("row_sum", [P, RING]), sb("row_inv", [P, RING])
                probs = sb("probs", [P, RING, 3 * P])
                probs_t = sb("probs_t", [P, NQT, HG, 3 * P])
                o_t = [sb(f"o_t_{n}", [P, C, SEQ], F32R) for n in ("hi", "lo")]
                o_new = [sb(f"o_new_{n}", [P, 2, SEQ], F32R) for n in ("hi", "lo")]
                res = sb("res", [P, 2, D])
                score_bank, turn_bank, o_bank, out_bank = psum[0:2], psum[2:4], psum[4:6], psum[6:8]

                def rounds2(eng, walk):
                    walk(attention_steps(True, False, True), 0)
                    with eng.Fori(1, B - 1) as b:
                        walk(attention_steps(True, True, True), b)
                    walk(attention_steps(True, True, False), B - 1)
                    walk(attention_steps(False, True, False), B)

                def done(b, per_batch, number):
                    return b * per_batch + (CREDIT + number + 1)

                def keys_of(t):
                    return (P if t == 0 else 0), (2 * P if t == NT - 1 else 3 * P)

                def unit(u):
                    tile, h = divmod(u, HG)
                    g, t = divmod(tile, NT)
                    return g, t, h

                def move_turned(eng, u, b):
                    g, t, h = unit(u)
                    lo, hi = keys_of(t)
                    wait_alone(eng, pv_done, done(b, TILES, u // HG - NQT + 1))
                    wait_alone(eng, transposed, done(b, UNITS, u))
                    dst = probs_t[:, t % NQT, h, lo:hi]
                    if u % 2 == 0:
                        eng.copy(dst, turn_bank[0][:, lo:hi]).then_inc(pt_by_act, 1)
                    else:
                        eng.tensor_copy(dst, turn_bank[1][:, lo:hi]).then_inc(pt_by_dve, 1)

                def o_place(part, g, half):
                    g %= C
                    cols = slice(half * HALF, half * HALF + HALF)
                    return o_new[part][:, g, cols] if g < 2 else o_t[part][:, g, cols]

                with nc.Block() as block:
                    @block.sync
                    def _(sp):
                        def walk(items, b):
                            here = b * SEQ if isinstance(b, int) else sp.snap(b * SEQ)
                            for it in items:
                                kind, args = it[0], it[1:]
                                if kind == "load_qk":
                                    g = args[0]
                                    token = here + SEQ * (g // C)
                                    wait_alone(sp, scores, done(b, UNITS, (g - 1) * GROUP - 1))
                                    f0 = g % C * P
                                    for q, parts_of in (("q", (0, 0, 1)), ("k", (0, 1, 0))):
                                        for row, part in enumerate(parts_of):
                                            src = qk_scratch[q][part, f0:f0 + P, bass.ds(token, SEQ)]
                                            sp.dma_start(stack[q][g % 2][DK * row:DK * row + DK].bitcast(F32),
                                                         src.rearrange("(h p) n -> p h n", p=DK)
                                                         ).then_inc(got_qk[g % 2], 16)
                                elif kind == "load_v":
                                    g = args[0]
                                    token = here + SEQ * (g // C)
                                    wait_alone(sp, pv_done, done(b, TILES, (g - 1) * NT - 1))
                                    f0 = g % C * P
                                    sp.dma_start(v_group[g % 2][:], v_scratch[bass.ds(token, SEQ), f0:f0 + P
                                                                              ].rearrange("(t p) d -> p t d", p=P)
                                                 ).then_inc(got_v[g % 2], 16)
                                elif kind == "o_move":
                                    wait_alone(sp, o_free, done(b, 2 * C, 3))
                                    wait_alone(sp, out_full, done(b, NT, -1))
                                    for part in range(2):
                                        sp.dma_start(o_t[part][:, 0:2, :].bitcast(F32),
                                                     o_new[part][:].bitcast(F32)).then_inc(o_moved, 16)
                                elif kind == "load_res":
                                    t = args[0]
                                    wait_alone(sp, stored[t % 2], b * (8 * NT) + (CREDIT + 16 * (t // 2) - 8 * NT))
                                    sp.dma_start(res[:, t % 2, :], xf[bass.ds(here + (t * P - SEQ), P), :]
                                                 ).then_inc(got_res[t % 2], 16)
                                elif kind == "store":
                                    t = args[0]
                                    wait_alone(sp, out_free, done(b, NT, t - NT))
                                    sp.dma_start(x2f[bass.ds(here + (t * P - SEQ), P), :],
                                                 res[:, t % 2, :]).then_inc(stored[t % 2], 16)

                        rounds2(sp, walk)
                        for s in stored:
                            sp.wait_ge(s, CREDIT + 8 * NT * B)

                    @block.gpsimd
                    def _(pool):
                        def walk(items, b):
                            for it in items:
                                kind, args = it[0], it[1:]
                                if kind == "norm":
                                    u = args[0]
                                    g, t, h = unit(u)
                                    lo, hi = keys_of(t)
                                    p = probs[:, u % RING, lo:hi]
                                    wait_alone(pool, inverted, done(b, UNITS // 2, u // 2))
                                    pool.tensor_scalar(p, p, row_inv[:, u % RING:u % RING + 1], 1.0,
                                                       ALU.mult, ALU.mult).then_inc(normed, 1)
                                elif kind == "res_bias":
                                    t = args[0]
                                    wait_alone(pool, got_res[t % 2], b * (8 * NT) + (16 * (t // 2 + 1) - 8 * NT))
                                    pool.tensor_tensor(res[:, t % 2, :], res[:, t % 2, :], bias_o[:],
                                                       ALU.add).then_inc(res_ready, 1)

                        rounds2(pool, walk)

                    @block.scalar
                    def _(act):
                        def walk(items, b):
                            for it in items:
                                kind, args = it[0], it[1:]
                                if kind == "score":
                                    u = args[0]
                                    g, t, h = unit(u)
                                    lo, hi = keys_of(t)
                                    act.wait_ge(transposed, done(b, UNITS, u - RING))
                                    act.wait_ge(masked, done(b, UNITS, u))
                                    act.activation(probs[:, u % RING, lo:hi], neg_scores[:, u % NSM, lo:hi], ACT.Exp,
                                                   bias=neg_max[:, u % RING:u % RING + 1], scale=-1.0,
                                                   accum_out=row_sum[:, u % RING:u % RING + 1]).then_inc(exped, 1)
                                elif kind == "turn" and args[0] % 2 == 0:
                                    move_turned(act, args[0], b)
                                elif kind == "o_evac":
                                    g, half = args
                                    if g not in (0, 1):
                                        act.wait_ge(out_full, done(b, NT, -1 if g > 0 else -1 - NT))
                                    elif not (isinstance(b, int) and b == 0):
                                        act.wait_ge(o_moved, b * 32)
                                    act.wait_ge(pv_done, done(b, TILES, g * NT + (NT // 2 if half == 0 else NT - 1)))
                                    act.copy(o_place(0, g, half), o_bank[half][:]).then_inc(o_hi, 1)

                        rounds2(act, walk)

                    @block.vector
                    def _(dve):
                        def walk(items, b):
                            for it in items:
                                kind, args = it[0], it[1:]
                                if kind == "score":
                                    u = args[0]
                                    g, t, h = unit(u)
                                    lo, hi = keys_of(t)
                                    wait_alone(dve, exped, done(b, UNITS, u - NSM))
                                    wait_alone(dve, scores, done(b, UNITS, u))
                                    dve.tensor_tensor_reduce(out=neg_scores[:, u % NSM, lo:hi],
                                                             in0=score_bank[u % 2][:, lo:hi], in1=window[:, lo:hi],
                                                             scale=-SCALE, scalar=BIG, op0=ALU.add, op1=ALU.min,
                                                             accum_out=neg_max[:, u % RING:u % RING + 1]
                                                             ).then_inc(masked, 1)
                                elif kind == "invert":
                                    u = 2 * args[0]
                                    wait_alone(dve, normed, done(b, UNITS, u + 1 - RING))
                                    wait_alone(dve, exped, done(b, UNITS, u + 1))
                                    dve.reciprocal(row_inv[:, u % RING:u % RING + 2],
                                                   row_sum[:, u % RING:u % RING + 2]).then_inc(inverted, 1)
                                elif kind == "turn" and args[0] % 2 == 1:
                                    move_turned(dve, args[0], b)
                                elif kind == "o_evac":
                                    g, half = args
                                    wait_alone(dve, o_hi, done(b, 2 * C, 2 * g + half))
                                    dve.tensor_tensor(o_place(1, g, half), o_bank[half][:],
                                                      o_place(0, g, half).bitcast(F32),
                                                      ALU.subtract).then_inc(o_free, 1)
                                elif kind == "out_evac":
                                    t = args[0]
                                    wait_alone(dve, res_ready, done(b, NT, t - NT))
                                    wait_alone(dve, out_full, done(b, NT, t - NT))
                                    dve.tensor_tensor(res[:, t % 2, :], out_bank[t % 2][:], res[:, t % 2, :],
                                                      ALU.add).then_inc(out_free, 1)

                        rounds2(dve, walk)

                    @block.tensor
                    def _(pe):
                        def walk(items, b):
                            for it in items:
                                kind, args = it[0], it[1:]
                                if kind == "score":
                                    u = args[0]
                                    g, t, h = unit(u)
                                    lo, hi = keys_of(t)
                                    if u % GROUP == 0:
                                        pe.wait_ge(got_qk[g % 2], b * (LOAD_QK * C // 2) + LOAD_QK * (g // 2 + 1))
                                    pe.wait_ge(masked, done(b, UNITS, u - 2))
                                    pe.matmul(score_bank[u % 2][:, lo:hi],
                                              stack["q"][g % 2][0:3 * DK, h, t * P:t * P + P],
                                              stack["k"][g % 2][0:3 * DK, h, (t - 1) * P + lo:(t - 1) * P + hi],
                                              start=True, stop=True).then_inc(scores, 1)
                                elif kind == "turn":
                                    u = args[0]
                                    g, t, h = unit(u)
                                    lo, hi = keys_of(t)
                                    moved = pt_by_act if u % 2 == 0 else pt_by_dve
                                    pe.wait_ge(moved, done(b, UNITS // 2, u // 2 - 1))
                                    pe.wait_ge(normed, done(b, UNITS, u))
                                    for col in range(lo, hi, P):
                                        last = pe.transpose(turn_bank[u % 2][:, col:col + P],
                                                            probs[:, u % RING, col:col + P], ident[:])
                                    last.then_inc(transposed, 1)
                                elif kind == "pv":
                                    g, k = divmod(args[0], NT)
                                    last_tile = g * NT + min(k + 1, NT - 1)
                                    for moved in (pt_by_act, pt_by_dve):
                                        pe.wait_ge(moved, done(b, UNITS // 2, (last_tile + 1) * HG // 2 - 1))
                                    if k == 0 or k == NT // 2 - 1:
                                        half = 0 if k == 0 else 1
                                        pe.wait_ge(o_free, done(b, 2 * C, 2 * g - 2 + half))
                                    if k == 0:
                                        pe.wait_ge(got_v[g % 2], b * (16 * C // 2) + 16 * (g // 2 + 1))
                                    for half in range(2):
                                        q0 = max(k - 1, half * NT // 2)
                                        q1 = min(k + 2, (half + 1) * NT // 2)
                                        if q0 >= q1:
                                            continue
                                        begins = k == 0 or (half == 1 and k == NT // 2 - 1)
                                        for h in range(HG):
                                            pieces = probs_t[:, q0 % NQT:q0 % NQT + q1 - q0, h, :]
                                            first_col = (k - q0 + 1) * P
                                            moving = diagonal(pieces, first_col, q1 - q0)
                                            col = (q0 * P) % HALF
                                            out_cols = o_bank[half][DK * h:DK * h + DK, col:col + (q1 - q0) * P]
                                            last = pe.matmul(out_cols.rearrange("p (q n) -> p q n", n=P),
                                                             v_group[g % 2][:, k, h * DK:(h + 1) * DK], moving,
                                                             start=begins, stop=True, skip_group_check=True)
                                    last.then_inc(pv_done, 1)
                                elif kind == "out":
                                    t, c_third = args
                                    bank = out_bank[t % 2]
                                    if c_third == 0:
                                        pe.wait_ge(o_moved, b * 32)
                                        pe.wait_ge(o_free, done(b, 2 * C, t // (NT // 2) - 2))
                                        pe.wait_ge(out_free, done(b, NT, t - NT - 2))
                                    products = [(c, a, v) for c in range(C) for a, v in PRODUCTS]
                                    for m in range(c_third * C, c_third * C + C):
                                        c, a, v = products[m]
                                        last = pe.matmul(bank[:], o_t[a][:, c, t * P:t * P + P], wo_w[v][:, c, :],
                                                         start=(m == 0), stop=(m == 3 * C - 1))
                                    if c_third == 2:
                                        last.then_inc(out_full, 1)

                        def diagonal(pieces, first_col, count):
                            ap = pieces[:, :, first_col:first_col + P]
                            if count == 1:
                                return ap
                            steps_ = [list(d) for d in ap.ap]
                            steps_[1][0] -= P
                            return bass.AP(tensor=ap.tensor, offset=ap.offset, ap=steps_)

                        rounds2(pe, walk)

        with ExitStack() as phase3:
            def sb(name, shape, dt=F32):
                return phase3.enter_context(nc.sbuf_tensor(name, shape, dt))

            keys_w = [sb(f"keys_{n}", [P, NE, C, P], F32R) for n in ("hi", "lo")]
            values_w = [sb(f"values_{n}", [P, NE, D], F32R) for n in ("hi", "lo")]
            sel_w = [sb(f"sel_{n}", [P, C, P], F32R) for n in ("hi", "lo")]

            with nc.sbuf_tensor("w_stage", [P, 2, 2048], F32) as w_stage, \
                    nc.sbuf_tensor("sel_raw", [NE, D], F32) as sel_raw:
                per_load = 4
                loads = [("keys", e) for e in range(0, NE, per_load)] + [("values", e) for e in range(0, NE, per_load)]

                def target(n, part):
                    what, e = loads[n]
                    if what == "keys":
                        return keys_w[part][:, e:e + per_load].rearrange("p e c h -> p (e c h)")
                    return values_w[part][:, e:e + per_load].rearrange("p e n -> p (e n)")

                with nc.Block() as block:
                    @block.sync
                    def _(sp):
                        sp.dma_start(sel_raw[:], sel).then_inc(got_weight, 16)
                        for n, (what, e) in enumerate(loads):
                            if n >= 2:
                                sp.wait_ge(split_lo, n - 1)
                            dst = w_stage[:, n % 2, :]
                            if what == "keys":
                                src = keys[e:e + per_load].rearrange("e (c p) h -> p (e c) h", p=P)
                                dst = dst.rearrange("p (ec h) -> p ec h", h=P)
                            else:
                                src = values[e:e + per_load].rearrange("e h n -> h e n")
                                dst = dst.rearrange("p (e n) -> p e n", n=D)
                            sp.dma_start(dst, src).then_inc(got_stage[n % 2], 16)

                    @block.scalar
                    def _(act):
                        for n in range(len(loads)):
                            act.wait_ge(got_stage[n % 2], 16 * (n // 2 + 1))
                            act.copy(target(n, 0), w_stage[:, n % 2, :]).then_inc(split_hi, 1)

                    @block.vector
                    def _(dve):
                        for part in range(2):
                            dve.memset(sel_w[part][:].bitcast(F32), 0.0).then_inc(sel_split, 1)
                        dve.wait_ge(sel_split, 2)
                        dve.wait_ge(sel_turned, 1)
                        turned = psum[0][:, 0:C * NE].rearrange("p (c e) -> p c e", c=C)
                        dve.tensor_copy(sel_w[0][:, :, 0:NE], turned).then_inc(sel_split, 1)
                        dve.wait_ge(sel_split, 3)
                        dve.tensor_tensor(sel_w[1][:, :, 0:NE], turned, sel_w[0][:, :, 0:NE].bitcast(F32),
                                          ALU.subtract).then_inc(sel_split, 1)
                        for n in range(len(loads)):
                            dve.wait_ge(split_hi, n + 1)
                            dve.tensor_tensor(target(n, 1), w_stage[:, n % 2, :], target(n, 0).bitcast(F32),
                                              ALU.subtract).then_inc(split_lo, 1)

                    @block.tensor
                    def _(pe):
                        pe.wait_ge(got_weight, 80)
                        for c in range(C):
                            last = pe.transpose(psum[0][:, c * NE:c * NE + NE], sel_raw[:, c * P:c * P + P],
                                                ident[0:NE, 0:NE])
                        last.then_inc(sel_turned, 1)

            x2 = [sb(f"x2_{par}", [P, TB, D]) for par in range(2)]
            x2_norm = sb("x2_norm", [P, 2, D])
            st2, mv2, rs2 = sb("st2", [P, 2, 6]), sb("mv2", [P, 2, 2]), sb("rs2", [P, 2, 1])
            x2_t = [[sb(f"x2_t{par}_{n}", [P, C, BLK], F32R) for n in ("hi", "lo")] for par in range(2)]
            gated_f = sb("gated_f", [P, 2, BLK])
            gated_w = [sb(f"gated_{n}", [P, 2, BLK], F32R) for n in ("hi", "lo")]
            gate_sb = sb("gate_sb", [P, 2, BLK])
            gates_t = [sb(f"gates_t{par}", [P, BLK], BF16) for par in range(2)]
            logits_sb = sb("logits_sb", [NE, BLK])
            exps = sb("exps", [P, TB, NE])
            router = sb("router", [P, TB, NE + TOPK])
            rest = sb("rest", [P, TB, NE + TOPK])
            top8, taken = sb("top8", [P, TB, 8]), sb("taken", [P, TB, 8])
            row = sb("row", [P, 4, TB])
            gates = sb("gates", [P, 3, TB, NE])
            parts = sb("parts", [P, TB, 3 * NE], BF16)
            out_bank, hidden_bank, gate_bank, misc_bank = psum[0:4], psum[4:6], psum[6], psum[7]
            ROUTE_OWN = 12 + TB * 3
            first3 = first_block_steps()
            steady3 = Steps(block_steps(0, False) + block_steps(1, False))
            final3 = Steps(block_steps(0, False) + block_steps(1, True))
            rounds3 = rounds_of(first3, steady3, final3, NB // 2 - 1)

            with nc.Block() as block:
                @block.sync
                def _(sp):
                    def walk(steps, n, b, is_first):
                        base = b * (2 * BLK) if isinstance(b, int) else sp.snap(b * (2 * BLK))
                        for it in steps.items:
                            kind, args = it[0], it[1:]
                            if kind == "load_x2":
                                par = args[0]
                                at = base if is_first else base + (BLK if par else 2 * BLK)
                                wait_alone(sp, out_stored[par], b * (16 * TB) + (CREDIT + (0 if is_first or par else 16 * TB)))
                                sp.dma_start(x2[par][:], x2f[bass.ds(at, BLK), :].rearrange("(t p) d -> p t d", p=P)
                                             ).then_inc(got_x2[par], 16)
                            elif kind == "final":
                                par, t = args
                                wait_alone(sp, finals, n.upto(it))
                                sp.dma_start(outf[bass.ds(base + (par * BLK + t * P), P), :],
                                             x2[par][:, t, :]).then_inc(out_stored[par], 16)

                    rounds3(sp, walk)
                    for s in out_stored:
                        sp.wait_ge(s, CREDIT + 16 * TB * (NB // 2))

                @block.gpsimd
                def _(pool):
                    def walk(steps, n, b, is_first):
                        for it in steps.items:
                            if it[0] == "ln3_rstd":
                                _, par, t = it
                                wait_alone(pool, stats3, n.upto(("ln3_stats", par, t)))
                                pool.tensor_tensor(rs2[:, t % 2, :], mv2[:, t % 2, 1:2], half_neg[:],
                                                   ALU.pow).then_inc(rstd3, 1)

                    rounds3(pool, walk)

                @block.scalar
                def _(act):
                    def walk(steps, n, b, is_first):
                        for it in steps.items:
                            kind, args = it[0], it[1:]
                            if kind == "gate":
                                par, e = args
                                act.wait_ge(gated, n.before("hidden") + (CREDIT + n.steps.ordinal[it] - 2))
                                act.wait_ge(gate_full, n.upto(it))
                                act.copy(gate_sb[:, e % 2, :], gate_bank[:]).then_inc(gate_ready, 1)
                            elif kind == "hidden":
                                par, e = args
                                act.wait_ge(value_done, n.ahead("value", it))
                                act.wait_ge(gated, n.upto(it))
                                act.copy(gated_w[0][:, e % 2, :], gated_f[:, e % 2, :]).then_inc(gated_hi, 1)
                            elif kind == "turn2_evac":
                                par, t = args
                                act.wait_ge(turned2, n.upto(("turn2", par, t)))
                                act.copy(x2_t[par][0][:, :, t * P:t * P + P],
                                         misc_bank[:].rearrange("p (c n) -> p c n", c=C)).then_inc(x2t_hi, 1)
                            elif kind == "sigmoid":
                                act.wait_ge(logits_tok, n.upto(("logits_turn", args[0])))
                                act.activation(exps[:].rearrange("p t e -> p (t e)"), misc_bank[:, 0:TB * NE],
                                               ACT.Exp, scale=-1.0).then_inc(router_exp, 1)

                    rounds3(act, walk)

                @block.vector
                def _(dve):
                    for m in (router, taken):
                        dve.memset(m[:], -1.0)
                    for par in range(2):
                        dve.memset(gates_t[par][:], 0.0)
                    dve.drain()

                    def walk(steps, n, b, is_first):
                        per_block = 2 * TB + ROUTE_OWN
                        before = 0 if is_first else per_block
                        k = 0

                        def link(*instructions):
                            nonlocal k
                            k += len(instructions)
                            for instruction in instructions:
                                instruction.then_inc(dve_linked, 1)
                            wait_alone(dve, dve_linked, b * (2 * per_block) + (before + k))

                        for it in steps.items:
                            kind, args = it[0], it[1:]
                            if kind == "ln3_stats":
                                par, t = args
                                if t == 0:
                                    wait_alone(dve, got_x2[par], b * 16 + (16 if is_first or par else 32))
                                link(dve.bn_stats(st2[:, t % 2, :], x2[par][:, t, :]))
                                link(dve.bn_aggr(mv2[:, t % 2, :], st2[:, t % 2, :]))
                                dve.tensor_scalar(mv2[:, t % 2, 1:2], mv2[:, t % 2, 1:2], EPS, None,
                                                  ALU.add).then_inc(stats3, 1)
                            elif kind == "ln3_apply":
                                par, t = args
                                wait_alone(dve, rstd3, n.upto(("ln3_rstd", par, t)))
                                dve.tensor_scalar(x2_norm[:, t % 2, :], x2[par][:, t, :], mv2[:, t % 2, 0:1],
                                                  rs2[:, t % 2, :], ALU.subtract, ALU.mult).then_inc(xn3, 1)
                            elif kind == "turn2_evac":
                                par, t = args
                                wait_alone(dve, x2t_hi, n.upto(it))
                                dve.tensor_tensor(x2_t[par][1][:, :, t * P:t * P + P],
                                                  misc_bank[:].rearrange("p (c n) -> p c n", c=C),
                                                  x2_t[par][0][:, :, t * P:t * P + P].bitcast(F32),
                                                  ALU.subtract).then_inc(x2t_ready, 1)
                            elif kind == "logits_evac":
                                wait_alone(dve, logits_done, n.upto(("logits", args[0])))
                                dve.tensor_copy(logits_sb[:], misc_bank[0:NE, :]).then_inc(logits_out, 1)
                            elif kind == "sigmoid":
                                wait_alone(dve, router_exp, n.upto(it))
                                link(dve.tensor_scalar(exps[:], exps[:], 1.0, None, ALU.add))
                                link(dve.reciprocal(router[:, :, 0:NE], exps[:]))
                                link(*[dve.max(top8[:, t, :], router[:, t, 0:NE]) for t in range(TB)])
                            elif kind == "choose":
                                link(dve.tensor_copy(taken[:, :, 0:TOPK], top8[:, :, 0:TOPK]),
                                     dve.reduce_sum(row[:, 0, :], top8[:, :, 0:TOPK], axis=AX_X))
                                replaced = [dve.match_replace(out=rest[:, t, :], in_to_replace=taken[:, t, :],
                                                              in_values=router[:, t, :], imm_value=0.0)
                                            for t in range(TB)]
                                link(*replaced, dve.tensor_scalar(row[:, 1, :], row[:, 0, :], 1e-9, None, ALU.max))
                                link(dve.reciprocal(row[:, 2, :], row[:, 1, :]))
                                link(dve.tensor_scalar(row[:, 3, :], row[:, 2, :], scale_col[:], None, ALU.mult),
                                     dve.tensor_tensor(gates[:, 0], router[:, :, 0:NE], rest[:, :, 0:NE],
                                                       ALU.subtract))
                            elif kind == "weigh":
                                link(*[dve.tensor_scalar(gates[:, 1, t, :], gates[:, 0, t, :], row[:, 3, t:t + 1],
                                                         None, ALU.mult) for t in range(TB)])
                                link(dve.tensor_copy(parts[:, :, 0:NE], gates[:, 1]))
                                link(dve.tensor_tensor(gates[:, 2], gates[:, 1], parts[:, :, 0:NE], ALU.subtract))
                                link(dve.tensor_copy(parts[:, :, NE:2 * NE], gates[:, 2]))
                                link(dve.tensor_tensor(gates[:, 0], gates[:, 2], parts[:, :, NE:2 * NE],
                                                       ALU.subtract))
                                dve.tensor_copy(parts[:, :, 2 * NE:3 * NE], gates[:, 0]).then_inc(gates_ready, 1)
                            elif kind == "gates_evac":
                                par = args[0]
                                wait_alone(dve, gates_turned, n.upto(("gates_turn", par)))
                                dve.tensor_copy(gates_t[par][0:3 * NE, :],
                                                misc_bank[0:3 * NE, 0:BLK // 2].bitcast(BF16)).then_inc(gates_out, 1)
                            elif kind == "hidden":
                                par, e = args
                                wait_alone(dve, gated_hi, n.upto(it, 2))
                                wait_alone(dve, gated_lo, n.upto(it, 2))
                                wait_alone(dve, gate_ready, n.upto(("gate", par, e)))
                                wait_alone(dve, hidden_full, n.upto(it))
                                dve.scalar_tensor_tensor(out=gated_f[:, e % 2, :], in0=hidden_bank[e % 2][:],
                                                         scalar=0.0, in1=gate_sb[:, e % 2, :], op0=ALU.max,
                                                         op1=ALU.mult).then_inc(gated, 1)
                                wait_alone(dve, value_done, n.ahead("value", it))
                                wait_alone(dve, gated_hi, n.upto(it))
                                dve.tensor_tensor(gated_w[1][:, e % 2, :], gated_f[:, e % 2, :],
                                                  gated_w[0][:, e % 2, :].bitcast(F32),
                                                  ALU.subtract).then_inc(gated_lo, 1)
                            elif kind == "final":
                                par, t = args
                                wait_alone(dve, value_done, n.upto(("value", par, NE - 1)))
                                dve.tensor_tensor(x2[par][:, t, :], out_bank[t][:], x2[par][:, t, :],
                                                  ALU.add).then_inc(finals, 1)

                    rounds3(dve, walk)

                @block.tensor
                def _(pe):
                    def walk(steps, n, b, is_first):
                        for it in steps.items:
                            kind, args = it[0], it[1:]
                            if kind == "gate":
                                par, e = args
                                pe.wait_ge(gate_ready, n.upto(it, 1))
                                if e == 0:
                                    pe.wait_ge(gates_out, n.upto(("gates_evac", par)))
                                pe.matmul(gate_bank[:], pick[:, e:e + 1].to_broadcast([P, P]), gates_t[par][:],
                                          start=True, stop=True).then_inc(gate_full, 1)
                            elif kind == "hidden":
                                par, e = args
                                pe.wait_ge(gated, n.upto(it, 2))
                                if e == 0:
                                    pe.wait_ge(x2t_ready, n.upto(("turn2_evac", par, TB - 1)))
                                for m, (c, a, m_x) in enumerate([(c, a, m_x) for c in range(C) for a, m_x in PRODUCTS]):
                                    last = pe.matmul(hidden_bank[e % 2][:], keys_w[a][:, e, c, :],
                                                     x2_t[par][m_x][:, c, :], start=(m == 0), stop=(m == 3 * C - 1))
                                last.then_inc(hidden_full, 1)
                            elif kind == "value":
                                par, e = args
                                pe.wait_ge(gated_hi, n.ahead("value", it) + 1)
                                pe.wait_ge(gated_lo, n.ahead("value", it) + 1)
                                for t in range(TB):
                                    if e == 0:
                                        pe.wait_ge(finals, n.ahead("final", it, TB - 1 - t))
                                    for m, (a, v) in enumerate(PRODUCTS):
                                        last = pe.matmul(out_bank[t][:], gated_w[a][:, e % 2, t * P:t * P + P],
                                                         values_w[v][:, e, :], start=(e == 0 and m == 0),
                                                         stop=(e == NE - 1 and m == 2))
                                last.then_inc(value_done, 1)
                            elif kind == "turn2":
                                par, t = args
                                pe.wait_ge(x2t_ready, n.ahead("turn2_evac", it))
                                pe.wait_ge(gates_out, n.ahead("gates_evac", it))
                                pe.wait_ge(xn3, n.upto(("ln3_apply", par, t)))
                                for c in range(C):
                                    last = pe.transpose(misc_bank[:, c * P:c * P + P],
                                                        x2_norm[:, t % 2, c * P:c * P + P], ident[:])
                                last.then_inc(turned2, 1)
                            elif kind == "logits":
                                par = args[0]
                                pe.wait_ge(x2t_ready, n.ahead("turn2_evac", it))
                                for m, (c, a, m_x) in enumerate([(c, a, m_x) for c in range(C) for a, m_x in PRODUCTS]):
                                    last = pe.matmul(misc_bank[:], sel_w[a][:, c, :], x2_t[par][m_x][:, c, :],
                                                     start=(m == 0), stop=(m == 3 * C - 1))
                                last.then_inc(logits_done, 1)
                            elif kind == "logits_turn":
                                wait_alone(pe, logits_out, n.upto(("logits_evac", args[0])))
                                for t in range(TB):
                                    last = pe.transpose(misc_bank[:, t * NE:t * NE + NE],
                                                        logits_sb[:, t * P:t * P + P], ident[0:NE, 0:NE])
                                last.then_inc(logits_tok, 1)
                            elif kind == "gates_turn":
                                wait_alone(pe, gates_ready, n.upto(("weigh", args[0])))
                                turned = misc_bank[0:3 * NE, 0:BLK // 2].bitcast(BF16)
                                for t in range(TB):
                                    last = pe.transpose(turned[:, t * P:t * P + P], parts[:, t, :], ident_bf[:])
                                last.then_inc(gates_turned, 1)

                    rounds3(pe, walk)


INPUTS = ["x", "ctx_1024", "L0_xattn_Wq", "L0_xattn_bq", "L0_xattn_Wk", "L0_xattn_bk", "L0_xattn_Wv", "L0_xattn_bv",
          "L0_xattn_Wo", "L0_xattn_bo", "L0_ffn_expert_sel", "L0_ffn_keys", "L0_ffn_values", "L0_ffn_route_scale"]


def kernel(**inputs):
    import numpy as np
    import concourse.bacc as bacc
    from concourse.bass_utils import run_bass_kernel_spmd

    nc = bacc.Bacc("TRN2", target_bir_lowering=False, num_devices=1)
    arrays, args = {}, []
    for name in INPUTS:
        a = np.ascontiguousarray(inputs[name])
        arrays[name + "_dram"] = a
        args.append(nc.dram_tensor(name + "_dram", a.shape, mybir.dt.from_np(a.dtype), kind="ExternalInput").ap())
    args.append(nc.dram_tensor("out_dram", (B, SEQ, D), F32, kind="ExternalOutput").ap())
    build_kernel(nc, *args)
    result = run_bass_kernel_spmd(nc, [arrays], core_ids=[0])
    return result.results[0]["out_dram"]
```

```python
from contextlib import ExitStack

import concourse.bass as bass
from concourse import mybir

ALU = mybir.AluOpType
ACT = mybir.ActivationFunctionType
F32 = mybir.dt.float32
F32R = mybir.dt.float32r
AX_X = mybir.AxisListType.X

P = 128
B, SEQ, D = 8, 1024, 512
HEADS, DK = 16, 32
C = D // P
NT = SEQ // P
HG = P // DK
GROUP = NT * HG
UNITS = C * GROUP
HALF = SEQ // 2
NE, TOPK = 16, 4
BLK = 512
NB = B * SEQ // BLK
TB = BLK // P
EPS = 1e-5
SCALE = 1.0 / float(DK) ** 0.5
MASKED = -1e30
BIG = 3e38
CREDIT = 64

LAG = 10
RING = 16
NSM = 4
NBUF = 3
NQT = 4
NBANK = 8
NSTAGE = 4
PRODUCTS = ((0, 0), (0, 1), (1, 0))
PV_STEPS = tuple((k, half, LAG + 1 + slot) for k, half, slot in (
    (0, 0, 8), (1, 0, 12), (2, 0, 16), (3, 0, 18), (4, 0, 20),
    (3, 1, 24), (4, 1, 26), (5, 1, 28), (6, 1, 32), (7, 1, 34)))
PV_TOTAL = C * len(PV_STEPS)
GATES_AHEAD, NGATE = 3, 4
PER_LOAD = 2
NWSTAGE = 4
HELD = 3
OUT_SLOTS = 14
OUT_PIECES = (0, 2, 4, 6, 8, 10)
LOAD_QK = 16 * 6
LOAD_IN = 16 * 2


class Steps:

    def __init__(self, items):
        self.items = items
        self.total = {}
        self.ordinal = {}
        self.seen = {}
        for it in items:
            self.seen[it] = dict(self.total)
            self.total[it[0]] = self.total.get(it[0], 0) + 1
            self.ordinal[it] = self.total[it[0]]


class Count:

    def __init__(self, steps, before):
        self.steps, self.before = steps, before

    def upto(self, item, back=0):
        return self.before(item[0]) + (CREDIT + self.steps.ordinal[item] - back)

    def ahead(self, kind, item, back=0):
        return self.before(kind) + (CREDIT + self.steps.seen[item].get(kind, 0) - back)


def leave(job):
    out = [] if job[0] == "v" else [("round", *job)]
    return out + [("evac", *job)] + ([("store", *job)] if job[0] in ("qk", "v") else [])


def project_steps(par, prepare_next, load_next):
    jobs = [("qk", par, g, q) for g in range(C) for q in "qk"] + [("v", par, t) for t in range(TB)]
    at = {}
    if prepare_next:
        for t in range(TB):
            at.setdefault(2 * t, []).extend([("ln_stats", 1 - par, t), ("ln_rstd", 1 - par, t)])
            at.setdefault(2 * t + 1, []).extend([("ln_apply", 1 - par, t), ("job", "tc", 1 - par, t)])
            at.setdefault(2 * t + 2, []).extend([("job", "tx", 1 - par, t)])
    items, waiting = [("load", par)] if load_next else [], []
    for n, job in enumerate(jobs):
        for it in at.pop(n, []) + [("job", *job)]:
            items.append(it)
            if it[0] == "job":
                for earlier in waiting:
                    items += leave(earlier)
                waiting = [it[1:]]
    assert not at
    return items + leave(waiting[0])


def first_project_steps():
    items = []
    for t, name in zip(range(TB), "qkvo"):
        items += [("ln_stats", 0, t), ("ln_rstd", 0, t), ("weight", name), ("ln_apply", 0, t)]
        items += [("job", "tc", 0, t), ("job", "tx", 0, t)] + leave(("tc", 0, t)) + leave(("tx", 0, t))
    return Steps(items + [("load", 1), ("settle",)])


def attention_steps(mine, after, ahead):
    at = {}

    def put(slot, *steps):
        at.setdefault(slot, []).extend(steps)

    def exists(n):
        return mine if n >= 0 else after

    if mine:
        if not after:
            put(-1, ("load_qk", 0), ("load_v", 0))
        for g in range(C if ahead else C - 1):
            put(g * GROUP + 3, ("load_qk", g + 1))
            put(g * GROUP + 14, ("load_v", g + 1))
        put(UNITS - 8, ("o_move",))
    if after:
        put(5, ("res_bias", 0))
        put(9, ("res_bias", 1))
        for t in range(NT):
            s0 = 8 + OUT_SLOTS * t
            for piece, slot in enumerate(OUT_PIECES):
                put(s0 + slot, ("out", t, piece))
            put(s0 + 11, ("out_evac", t), ("store", t))
            if t + 2 < NT or mine:
                put(s0 + 11, ("load_res", t + 2))
            if t + 2 < NT:
                put(s0 + 20, ("res_bias", t + 2))
    else:
        put(UNITS - 20, ("load_res", NT), ("load_res", NT + 1))
    for g in range(-1, C):
        if exists(g):
            for k, half, slot in PV_STEPS:
                steps = [(slot, ("pv", g, k, half))]
                if (k, half) in ((NT // 2, 0), (NT - 1, 1)):
                    steps += [(slot, ("o_hi", g, half)), (slot + 1, ("o_lo", g, half))]
                for when, step in steps:
                    if 0 <= g * GROUP + when < UNITS:
                        put(g * GROUP + when, step)
    items = []
    for s in range(-1, UNITS):
        if s >= 0:
            if mine:
                items += [("score", s)]
            if s % 2 and exists(s - 3):
                items += [("invert", (s - 3) // 2), ("norm", s - 3), ("norm", s - 2)]
            if exists(s - LAG):
                items += [("turn", s - LAG)]
        items += at.pop(s, [])
        if s >= 0 and mine:
            items += [("exp", s)]
    assert not at
    return items


def prepare(par, t):
    return [("ln3_stats", par, t), ("ln3_rstd", par, t), ("ln3_apply", par, t)]


ROUTE = ("logits", "logits_evac", "logits_turn", "sigmoid", "choose", "weigh", "gates_turn", "gates_evac",
         "gate_store")


def block_steps(par, last):
    at = {}
    if not last:
        for t in range(TB):
            at.setdefault(t + 2, []).extend(prepare(1 - par, t))
            at.setdefault(t + 3, []).extend([("turn2", 1 - par, t), ("turn2_evac", 1 - par, t)])
        for kind, e in zip(ROUTE, (7, 7, 8, 9, 10, 11, 12, 12, 12)):
            at.setdefault(e, []).append((kind, 1 - par))
    items = [] if last else [("load_x2", 1 - par)]
    for e in range(NE):
        if e + GATES_AHEAD < NE:
            items += [("gate", par, e + GATES_AHEAD)]
        elif not last:
            items += [("gate", 1 - par, e + GATES_AHEAD - NE)]
        if e + 1 < NE:
            items += [("hidden", par, e + 1)]
        elif not last:
            items += [("hidden", 1 - par, 0)]
        items += [("value", par, e)] + at.pop(e, [])
    assert not at
    return items + [("final", par, t) for t in range(TB)]


def first_block_steps():
    splits = iter([("split", what, e) for e in range(0, NE, PER_LOAD) for what in ("keys", "values")])
    items = [("load_x2", 0)]
    for t in range(TB + 1):
        if t < TB:
            items += prepare(0, t)[:2] + [next(splits)]
            if t:
                items += [next(splits)]
        if t:
            items += [("turn2_evac", 0, t - 1)]
        if t < TB:
            items += prepare(0, t)[2:] + [("turn2", 0, t)]
    for kind in ROUTE:
        items += [next(splits), (kind, 0)] if kind not in ("logits_turn", "weigh", "gate_store") else [(kind, 0)]
    items += [("gate", 0, 0), ("gate", 0, 1), *splits, ("gate", 0, 2), ("hidden", 0, 0), ("settle",)]
    return Steps(items)


def build_kernel(nc, x, ctx_in, wq, bq, wk, bk, wv, bv, wo, bo, sel, keys, values, route_scale, out):
    xf = x.rearrange("b s d -> (b s) d")
    cf = ctx_in.rearrange("b s d -> (b s) d")
    outf = out.rearrange("b s d -> (b s) d")
    x2f = nc.dram_tensor("x2_scratch", (B * SEQ, D), F32, kind="Internal").ap()
    qk_scratch = {q: nc.dram_tensor(f"{q}_scratch", (2, D, B * SEQ), F32, kind="Internal").ap() for q in "qk"}
    gate_scratch = [nc.dram_tensor(f"gate_scratch{par}", (NE, BLK), F32, kind="Internal").ap() for par in range(2)]
    v_scratch = nc.dram_tensor("v_scratch", (B * SEQ, D), F32, kind="Internal").ap()

    with ExitStack() as whole:
        def sem(name):
            return whole.enter_context(nc.semaphore(name))

        psum = [whole.enter_context(nc.psum_tensor(f"bank{i}", [P, 512], F32)) for i in range(8)]

        def wait_alone(eng, semaphore, value):
            eng.wait_ge(semaphore, value)
            if not isinstance(value, int) and eng.engine in waited:
                eng.sem_inc(waited[eng.engine], 1)

        def rounds_of(first, steady, final, count):
            def rounds(eng, walk):
                def before(b):
                    return lambda k: b * steady.total.get(k, 0) + first.total.get(k, 0)
                walk(first, Count(first, lambda k: 0), 0, True)
                with eng.Fori(0, count) as b:
                    walk(steady, Count(steady, before(b)), b, False)
                walk(final, Count(final, before(count)), count, False)
            return rounds

        waited = {nc.gpsimd.engine: sem("pool_waited"), nc.vector.engine: sem("dve_waited"),
                  nc.sync.engine: sem("sp_waited"), nc.tensor.engine: sem("pe_waited")}
        stats_done, rstd_done, xn_ready = sem("stats_done"), sem("rstd_done"), sem("xn_ready")
        job_full, job_hi, job_free = sem("job_full"), sem("job_hi"), sem("job_free")
        scores, masked, exped = sem("scores"), sem("masked"), sem("exped")
        inverted, normed = sem("inverted"), sem("normed")
        transposed, pt_by_act, pt_by_dve = sem("transposed"), sem("pt_by_act"), sem("pt_by_dve")
        pv_done, o_hi, o_free = sem("pv_done"), sem("o_hi"), sem("o_free")
        out_full, out_free, res_ready = sem("out_full"), sem("out_free"), sem("res_ready")
        stats3, rstd3, xn3 = sem("stats3"), sem("rstd3"), sem("xn3")
        turned2, x2t_hi, x2t_ready = sem("turned2"), sem("x2t_hi"), sem("x2t_ready")
        logits_done, logits_out, logits_tok = sem("logits_done"), sem("logits_out"), sem("logits_tok")
        router_exp, gates_ready, gates_turned, gates_out = (
            sem("router_exp"), sem("gates_ready"), sem("gates_turned"), sem("gates_out"))
        hidden_full = sem("hidden_full")
        gated, gated_hi, gated_lo, value_done = sem("gated"), sem("gated_hi"), sem("gated_lo"), sem("value_done")
        finals = sem("finals")
        got_const, got_weight = sem("got_const"), {n: sem(f"got_weight_{n}") for n in "qkvo"}
        got_in = [sem(f"got_in{i}") for i in range(2)]
        qk_stored = [sem(f"qk_stored{i}") for i in range(NSTAGE)]
        v_stored = [sem(f"v_stored{i}") for i in range(2)]
        got_qk = [sem(f"got_qk{i}") for i in range(2)]
        got_v = [sem(f"got_v{i}") for i in range(2)]
        o_moved = sem("o_moved")
        got_res = [sem(f"got_res{i}") for i in range(2)]
        stored = [sem(f"stored{i}") for i in range(2)]
        got_x2 = [sem(f"got_x2_{i}") for i in range(2)]
        gate_stored = [sem(f"gate_stored{i}") for i in range(2)]
        got_gate = [sem(f"got_gate{i}") for i in range(NGATE)]
        out_stored = [sem(f"out_stored{i}") for i in range(2)]
        credits = [stats_done, rstd_done, xn_ready, job_full, job_hi, job_free, *qk_stored, *v_stored,
                   scores, masked, exped, inverted, normed, transposed, pt_by_act, pt_by_dve, pv_done, o_hi,
                   o_free, out_full, out_free, res_ready, *stored, *out_stored,
                   stats3, rstd3, xn3, turned2, x2t_hi, x2t_ready, logits_done, logits_out, logits_tok,
                   router_exp, gates_ready, gates_turned, gates_out, hidden_full,
                   gated, gated_hi, gated_lo, value_done, finals]
        dve_own, dve_linked, pool_own = sem("dve_own"), sem("dve_linked"), sem("pool_own")
        weight_hi, weight_lo, weight_lo_pool = sem("weight_hi"), sem("weight_lo"), sem("weight_lo_pool")
        split_hi, split_lo, got_stage = sem("split_hi"), sem("split_lo"), [sem(f"got_stage{i}") for i in range(NWSTAGE)]
        got_sel, sel_turned, sel_split = sem("got_sel"), sem("sel_turned"), sem("sel_split")
        ident_ready = sem("ident_ready")
        ident = whole.enter_context(nc.sbuf_tensor("ident", [P, P], F32))
        half_neg = whole.enter_context(nc.sbuf_tensor("half_neg", [P, 1], F32))
        sel_t = whole.enter_context(nc.sbuf_tensor("sel_t", [P, C, NE], F32))
        scale_col = whole.enter_context(nc.sbuf_tensor("scale_col", [P, 1], F32))

        with ExitStack() as attention:
            wo_w = [attention.enter_context(nc.sbuf_tensor(f"wo_{n}", [P, C, D], F32R)) for n in ("hi", "lo")]
            bias_o = attention.enter_context(nc.sbuf_tensor("bias_o", [P, D], F32))
            window = attention.enter_context(nc.sbuf_tensor("window", [P, 3 * P], F32))

            with ExitStack() as phase1:
                def sb(name, shape, dt=F32):
                    return phase1.enter_context(nc.sbuf_tensor(name, shape, dt))

                w = {n: [sb(f"w{n}_{part}", [P, C, D], F32R) for part in ("hi", "lo")] for n in "qkv"}
                w["o"] = wo_w
                bias = {n: sb(f"bias_{n}", [P, C]) for n in "qk"}
                bias_v = sb("bias_v", [P, D])

                x_in = [sb(f"x_in{par}", [P, TB, D]) for par in range(2)]
                c_in = [sb(f"c_in{par}", [P, TB, D]) for par in range(2)]
                v_raw = sb("v_raw", [P, C, D])
                raw = {"q": x_in[1], "k": c_in[1], "v": v_raw, "o": v_raw}

                def load_weight(sp, name):
                    src = {"q": wq, "k": wk, "v": wv, "o": wo}[name]
                    sp.dma_start(raw[name][:], src.rearrange("(c p) n -> p c n", p=P)).then_inc(got_weight[name], 16)

                with nc.sbuf_tensor("sel_raw", [NE, D], F32) as sel_raw, nc.Block() as block:
                    @block.sync
                    def _(sp):
                        sp.dma_start(sel_raw[:], sel).then_inc(got_sel, 16)
                        for dst, src in ((x_in, xf), (c_in, cf)):
                            sp.dma_start(dst[0][:], src[0:BLK, :].rearrange("(t p) d -> p t d", p=P)
                                         ).then_inc(got_in[0], 16)
                        for name in "qkv":
                            load_weight(sp, name)
                        for n, src in (("q", bq), ("k", bk)):
                            sp.dma_start(bias[n][:], src.rearrange("(c p) -> p c", p=P),
                                         allow_slow_non_contiguous=True).then_inc(got_const, 16)
                        sp.dma_start(bias_v[:], bv.partition_broadcast(P)).then_inc(got_const, 16)
                        sp.dma_start(bias_o[:], bo.partition_broadcast(P)).then_inc(got_const, 16)
                        sp.dma_start(scale_col[:], route_scale.partition_broadcast(P)).then_inc(got_const, 16)

                    @block.vector
                    def _(dve):
                        dve.wait_ge(sel_turned, 1)
                        dve.tensor_copy(sel_t[:], psum[0][:, 0:C * NE].rearrange("p (c e) -> p c e", c=C))
                        dve.drain()

                    @block.tensor
                    def _(pe):
                        pe.wait_ge(ident_ready, 1)
                        pe.wait_ge(got_sel, 16)
                        for c in range(C):
                            last = pe.transpose(psum[0][:, c * NE:c * NE + NE], sel_raw[:, c * P:c * P + P],
                                                ident[0:NE, 0:NE])
                        last.then_inc(sel_turned, 1)

                    @block.gpsimd
                    def _(pool):
                        for s in credits:
                            pool.sem_inc(s, CREDIT)
                        pool.memset(half_neg[:], -0.5)
                        pool.memset(ident[:], 0.0).then_inc(pool_own, 1)
                        pool.memset(window[:], 0.0).then_inc(pool_own, 1)
                        pool.wait_ge(pool_own, 2)
                        pool.affine_select(out=ident[:], in_=ident[:], compare_op=ALU.not_equal, fill=1.0, base=0,
                                           pattern=[[-1, P]], channel_multiplier=1).then_inc(ident_ready, 1)
                        pool.affine_select(out=window[:], in_=window[:], compare_op=ALU.is_ge, fill=MASKED, base=0,
                                           pattern=[[1, 3 * P]], channel_multiplier=-1).then_inc(pool_own, 1)
                        pool.wait_ge(pool_own, 3)
                        pool.affine_select(out=window[:], in_=window[:], compare_op=ALU.is_ge, fill=MASKED,
                                           base=2 * P, pattern=[[-1, 3 * P]],
                                           channel_multiplier=1).then_inc(pool_own, 1)
                        pool.wait_ge(pool_own, 4)

                x_norm = sb("x_norm", [P, 2, D])
                ln_st, ln_mv, ln_rs = sb("ln_st", [P, 2, 6]), sb("ln_mv", [P, 2, 2]), sb("ln_rs", [P, 2, 1])
                x_t = [[sb(f"x_t{par}_{n}", [P, C, BLK], F32R) for n in ("hi", "lo")] for par in range(2)]
                c_t = [[sb(f"c_t{par}_{n}", [P, C, BLK], F32R) for n in ("hi", "lo")] for par in range(2)]
                qk_stage = sb("qk_stage", [P, NSTAGE, 2, BLK], F32R)
                v_stage = sb("v_stage", [P, 2, D])

                first1 = first_project_steps()
                steady1 = Steps(project_steps(0, True, True) + project_steps(1, True, True))
                final1 = Steps(project_steps(0, True, False) + project_steps(1, False, False))
                rounds1 = rounds_of(first1, steady1, final1, NB // 2 - 1)
                assert first1.total["job"] % NBANK == 0 and steady1.total["job"] % NBANK == 0
                evacs = [it[1:] for it in project_steps(0, True, True) if it[0] == "evac"]
                behind_turns = len(evacs) - 1 - evacs.index(("tx", 1, TB - 1))

                def job_bank(n, job):
                    return psum[(n.steps.ordinal[("job", *job)] - 1) % NBANK]

                def qk_slot(par, g, q):
                    number = (par * C + g) * 2 + "qk".index(q)
                    return number, number % NSTAGE

                with nc.Block() as block:
                    @block.sync
                    def _(sp):
                        def walk(steps, n, b, is_first):
                            base = b * (2 * BLK) if isinstance(b, int) else sp.snap(b * (2 * BLK))
                            for it in steps.items:
                                kind, args = it[0], it[1:]
                                if kind == "load":
                                    par = args[0]
                                    at = base + par * BLK + (0 if is_first else 2 * BLK)
                                    if is_first:
                                        sp.wait_ge(weight_lo, 2)
                                    else:
                                        wait_alone(sp, xn_ready, n.ahead("ln_apply", it))
                                        wait_alone(sp, job_full, n.ahead("job", it))
                                    for dst, src in ((x_in, xf), (c_in, cf)):
                                        sp.dma_start(dst[par][:], src[bass.ds(at, BLK), :].rearrange(
                                            "(t p) d -> p t d", p=P)).then_inc(got_in[par], 16)
                                elif it == ("weight", "o"):
                                    sp.wait_ge(weight_lo_pool, 1)
                                    load_weight(sp, "o")
                                elif kind == "store" and args[0] == "qk":
                                    _, par, g, q = args
                                    _, slot = qk_slot(par, g, q)
                                    wait_alone(sp, job_free, n.upto(("evac", *args)))
                                    sp.dma_start(qk_scratch[q][:, g * P:g * P + P, bass.ds(base + par * BLK, BLK)
                                                               ].rearrange("a p n -> p a n"),
                                                 qk_stage[:, slot].bitcast(F32)).then_inc(qk_stored[slot], 16)
                                elif kind == "store":
                                    _, par, t = args
                                    wait_alone(sp, job_free, n.upto(("evac", *args)))
                                    sp.dma_start(v_scratch[bass.ds(base + (par * BLK + t * P), P), :],
                                                 v_stage[:, t % 2, :]).then_inc(v_stored[t % 2], 16)

                        rounds1(sp, walk)
                        for s in qk_stored:
                            sp.wait_ge(s, CREDIT + 16 * (2 * C // NSTAGE) * NB)
                        for s in v_stored:
                            sp.wait_ge(s, CREDIT + 16 * (TB // 2) * NB)

                    @block.gpsimd
                    def _(pool):
                        def walk(steps, n, b, is_first):
                            for it in steps.items:
                                if it[0] == "weight" and it[1] in "vo":
                                    name = it[1]
                                    pool.wait_ge(weight_hi, "qkvo".index(name) + 1)
                                    pool.tensor_tensor(w[name][1][:], raw[name][:], w[name][0][:].bitcast(F32),
                                                       ALU.subtract).then_inc(weight_lo_pool, 1)
                                elif it[0] == "ln_rstd":
                                    _, par, t = it
                                    wait_alone(pool, stats_done, n.upto(("ln_stats", par, t)))
                                    pool.tensor_tensor(ln_rs[:, t % 2, :], ln_mv[:, t % 2, 1:2], half_neg[:],
                                                       ALU.pow).then_inc(rstd_done, 1)

                        rounds1(pool, walk)

                    @block.scalar
                    def _(act):
                        def walk(steps, n, b, is_first):
                            for it in steps.items:
                                kind, args = it[0], it[1:]
                                if kind == "weight":
                                    name = args[0]
                                    act.wait_ge(got_weight[name], 16)
                                    act.copy(w[name][0][:], raw[name][:]).then_inc(weight_hi, 1)
                                if kind == "settle":
                                    act.wait_ge(got_const, 80)
                                if kind != "round":
                                    continue
                                bank = job_bank(n, args)
                                if args[0] == "qk":
                                    _, par, g, q = args
                                    number, slot = qk_slot(par, g, q)
                                    act.wait_ge(qk_stored[slot], b * (16 * 4 * C // NSTAGE)
                                                + (CREDIT + 16 * (number // NSTAGE)))
                                    act.wait_ge(job_full, n.upto(("job", *args)))
                                    act.activation(qk_stage[:, slot, 0, :], bank[:], ACT.Identity,
                                                   bias=bias[q][:, g:g + 1]).then_inc(job_hi, 1)
                                else:
                                    what, par, t = args
                                    dst = (x_t if what == "tx" else c_t)[par][0]
                                    act.wait_ge(job_full, n.upto(("job", *args)))
                                    act.copy(dst[:, :, t * P:t * P + P],
                                             bank[:].rearrange("p (c n) -> p c n", c=C)).then_inc(job_hi, 1)

                        rounds1(act, walk)

                    @block.vector
                    def _(dve):
                        def walk(steps, n, b, is_first):
                            k = 0 if is_first else 2 * TB

                            def link(instruction):
                                nonlocal k
                                k += 1
                                instruction.then_inc(dve_own, 1)
                                wait_alone(dve, dve_own, b * (4 * TB) + k)

                            for it in steps.items:
                                kind, args = it[0], it[1:]
                                if kind == "weight" and args[0] in "qk":
                                    name = args[0]
                                    dve.wait_ge(weight_hi, "qkvo".index(name) + 1)
                                    dve.tensor_tensor(w[name][1][:], raw[name][:], w[name][0][:].bitcast(F32),
                                                      ALU.subtract).then_inc(weight_lo, 1)
                                elif kind == "settle":
                                    dve.wait_ge(got_const, 80)
                                elif kind == "ln_stats":
                                    par, t = args
                                    if t == 0:
                                        wait_alone(dve, got_in[par], b * LOAD_IN + (
                                            LOAD_IN if is_first or par else 2 * LOAD_IN))
                                    link(dve.bn_stats(ln_st[:, t % 2, :], x_in[par][:, t, :]))
                                    link(dve.bn_aggr(ln_mv[:, t % 2, :], ln_st[:, t % 2, :]))
                                    dve.tensor_scalar(ln_mv[:, t % 2, 1:2], ln_mv[:, t % 2, 1:2], EPS, None,
                                                      ALU.add).then_inc(stats_done, 1)
                                elif kind == "ln_apply":
                                    par, t = args
                                    wait_alone(dve, rstd_done, n.upto(("ln_rstd", par, t)))
                                    dve.tensor_scalar(x_norm[:, t % 2, :], x_in[par][:, t, :], ln_mv[:, t % 2, 0:1],
                                                      ln_rs[:, t % 2, :], ALU.subtract, ALU.mult).then_inc(xn_ready, 1)
                                elif kind == "evac" and args[0] == "qk":
                                    _, par, g, q = args
                                    _, slot = qk_slot(par, g, q)
                                    wait_alone(dve, job_hi, n.upto(("round", *args)))
                                    dve.scalar_tensor_tensor(out=qk_stage[:, slot, 1, :], in0=job_bank(n, args)[:],
                                                             scalar=bias[q][:, g:g + 1],
                                                             in1=qk_stage[:, slot, 0, :].bitcast(F32),
                                                             op0=ALU.add, op1=ALU.subtract).then_inc(job_free, 1)
                                elif kind == "evac" and args[0] == "v":
                                    _, par, t = args
                                    wait_alone(dve, v_stored[t % 2], b * (16 * TB) + (
                                        CREDIT + 16 * ((par * TB + t) // 2)))
                                    wait_alone(dve, job_full, n.upto(("job", *args)))
                                    dve.tensor_tensor(v_stage[:, t % 2, :], job_bank(n, args)[:], bias_v[:],
                                                      ALU.add).then_inc(job_free, 1)
                                elif kind == "evac":
                                    what, par, t = args
                                    hi, lo = (x_t if what == "tx" else c_t)[par]
                                    wait_alone(dve, job_hi, n.upto(("round", *args)))
                                    dve.tensor_tensor(lo[:, :, t * P:t * P + P],
                                                      job_bank(n, args)[:].rearrange("p (c n) -> p c n", c=C),
                                                      hi[:, :, t * P:t * P + P].bitcast(F32),
                                                      ALU.subtract).then_inc(job_free, 1)

                        rounds1(dve, walk)

                    @block.tensor
                    def _(pe):
                        def walk(steps, n, b, is_first):
                            for it in steps.items:
                                kind, args = it[0], it[1:]
                                if kind == "settle":
                                    pe.wait_ge(job_free, CREDIT + 2 * TB)
                                    pe.wait_ge(weight_lo, 2)
                                    pe.wait_ge(weight_lo_pool, 1)
                                if kind != "job":
                                    continue
                                bank = job_bank(n, args)
                                pe.wait_ge(job_free, n.before("evac") + (CREDIT + n.steps.ordinal[it] - NBANK))
                                if args[0] == "tx":
                                    _, par, t = args
                                    pe.wait_ge(xn_ready, n.upto(("ln_apply", par, t)))
                                    for c in range(C):
                                        last = pe.transpose(bank[:, c * P:c * P + P],
                                                            x_norm[:, t % 2, c * P:c * P + P], ident[:])
                                elif args[0] == "tc":
                                    _, par, t = args
                                    if t == 0:
                                        pe.wait_ge(got_in[par], b * LOAD_IN + (
                                            LOAD_IN if is_first or par else 2 * LOAD_IN))
                                    for c in range(C):
                                        last = pe.transpose(bank[:, c * P:c * P + P],
                                                            c_in[par][:, t, c * P:c * P + P], ident[:])
                                elif args[0] == "qk":
                                    _, par, g, q = args
                                    src = (x_t if q == "q" else c_t)[par]
                                    if g == 0 and q == "q":
                                        pe.wait_ge(job_free, n.ahead("evac", it, behind_turns))
                                    for m, (c, a, s) in enumerate([(c, a, s) for c in range(C) for a, s in PRODUCTS]):
                                        last = pe.matmul(bank[:], w[q][a][:, c, g * P:g * P + P], src[s][:, c, :],
                                                         start=(m == 0), stop=(m == 3 * C - 1))
                                else:
                                    _, par, t = args
                                    for m, (c, s, a) in enumerate([(c, s, a) for c in range(C) for s, a in PRODUCTS]):
                                        last = pe.matmul(bank[:], c_t[par][s][:, c, t * P:t * P + P],
                                                         w["v"][a][:, c, :], start=(m == 0), stop=(m == 3 * C - 1))
                                last.then_inc(job_full, 1)

                        rounds1(pe, walk)

            with ExitStack() as phase2:
                def sb(name, shape, dt=F32):
                    return phase2.enter_context(nc.sbuf_tensor(name, shape, dt))

                stack = {q: [sb(f"stack_{q}{i}", [P, HG, SEQ], F32R) for i in range(2)] for q in "qk"}
                v_group = [sb(f"v_group{i}", [P, NT, P]) for i in range(2)]
                neg_scores = sb("neg_scores", [P, NSM, 3 * P])
                neg_max, row_sum, row_inv = sb("neg_max", [P, RING]), sb("row_sum", [P, RING]), sb("row_inv", [P, RING])
                probs = sb("probs", [P, RING, 3 * P])
                probs_t = sb("probs_t", [P, NQT, HG, 3 * P])
                o_t = [sb(f"o_t_{n}", [P, C, SEQ], F32R) for n in ("hi", "lo")]
                o_new = [sb(f"o_new_{n}", [P, HELD, SEQ], F32R) for n in ("hi", "lo")]
                res = sb("res", [P, 2, D])
                score_bank, turn_bank, o_bank, out_bank = psum[0:NBUF], psum[NBUF:2 * NBUF], psum[6], psum[7]

                def rounds2(eng, walk):
                    walk(attention_steps(True, False, True), 0)
                    with eng.Fori(1, B - 1) as b:
                        walk(attention_steps(True, True, True), b)
                    walk(attention_steps(True, True, False), B - 1)
                    walk(attention_steps(False, True, False), B)

                def done(b, per_batch, number):
                    return b * per_batch + (CREDIT + number + 1)

                def keys_of(t):
                    return (P if t == 0 else 0), (2 * P if t == NT - 1 else 3 * P)

                def unit(u):
                    tile, h = divmod(u, HG)
                    g, t = divmod(tile, NT)
                    return g, t, h

                def ring_slot(u):
                    return u % UNITS % NBUF

                def earlier_in_ring(u):
                    return next(e for e in range(u - 1, u - 2 * NBUF, -1) if ring_slot(e) == ring_slot(u))

                def pv_number(g, k, half):
                    return g * len(PV_STEPS) + [step[:2] for step in PV_STEPS].index((k, half))

                def last_reader(tile):
                    g, t = divmod(tile, NT)
                    return pv_number(g, min(t + 1, NT - 1, NT // 2 if t < NT // 2 else NT), t // (NT // 2))

                def move_turned(eng, u, b):
                    g, t, h = unit(u)
                    lo, hi = keys_of(t)
                    wait_alone(eng, pv_done, done(b, PV_TOTAL, last_reader(u // HG - NQT)))
                    wait_alone(eng, transposed, done(b, UNITS, u))
                    dst = probs_t[:, t % NQT, h, lo:hi]
                    if u % 2 == 0:
                        eng.copy(dst, turn_bank[ring_slot(u)][:, lo:hi]).then_inc(pt_by_act, 1)
                    else:
                        eng.tensor_copy(dst, turn_bank[ring_slot(u)][:, lo:hi]).then_inc(pt_by_dve, 1)

                def out_place(t, b):
                    return score_bank[0] if isinstance(b, int) and b == B and t % 2 else out_bank

                def o_place(part, g, half):
                    g %= C
                    cols = slice(half * HALF, half * HALF + HALF)
                    return o_new[part][:, g, cols] if g < HELD else o_t[part][:, g, cols]

                with nc.Block() as block:
                    @block.sync
                    def _(sp):
                        def walk(items, b):
                            here = b * SEQ if isinstance(b, int) else sp.snap(b * SEQ)
                            for it in items:
                                kind, args = it[0], it[1:]
                                if kind == "load_qk":
                                    g = args[0]
                                    token = here + SEQ * (g // C)
                                    wait_alone(sp, scores, done(b, UNITS, (g - 1) * GROUP - 1))
                                    f0 = g % C * P
                                    for q, parts_of in (("q", (0, 0, 1)), ("k", (0, 1, 0))):
                                        for row, part in enumerate(parts_of):
                                            src = qk_scratch[q][part, f0:f0 + P, bass.ds(token, SEQ)]
                                            sp.dma_start(stack[q][g % 2][DK * row:DK * row + DK].bitcast(F32),
                                                         src.rearrange("(h p) n -> p h n", p=DK)
                                                         ).then_inc(got_qk[g % 2], 16)
                                elif kind == "load_v":
                                    g = args[0]
                                    token = here + SEQ * (g // C)
                                    wait_alone(sp, pv_done, done(b, PV_TOTAL, pv_number(g - 2, NT - 1, 1)))
                                    f0 = g % C * P
                                    sp.dma_start(v_group[g % 2][:], v_scratch[bass.ds(token, SEQ), f0:f0 + P
                                                                              ].rearrange("(t p) d -> p t d", p=P)
                                                 ).then_inc(got_v[g % 2], 16)
                                elif kind == "o_move":
                                    wait_alone(sp, o_free, done(b, 2 * C, 2 * HELD - 1))
                                    wait_alone(sp, out_full, done(b, NT, -1))
                                    for part in range(2):
                                        sp.dma_start(o_t[part][:, 0:HELD, :].bitcast(F32),
                                                     o_new[part][:].bitcast(F32)).then_inc(o_moved, 16)
                                elif kind == "load_res":
                                    t = args[0]
                                    wait_alone(sp, stored[t % 2], b * (8 * NT) + (CREDIT + 16 * (t // 2) - 8 * NT))
                                    sp.dma_start(res[:, t % 2, :], xf[bass.ds(here + (t * P - SEQ), P), :]
                                                 ).then_inc(got_res[t % 2], 16)
                                elif kind == "store":
                                    t = args[0]
                                    wait_alone(sp, out_free, done(b, NT, t - NT))
                                    sp.dma_start(x2f[bass.ds(here + (t * P - SEQ), P), :],
                                                 res[:, t % 2, :]).then_inc(stored[t % 2], 16)

                        rounds2(sp, walk)
                        for s in stored:
                            sp.wait_ge(s, CREDIT + 8 * NT * B)

                    @block.gpsimd
                    def _(pool):
                        def walk(items, b):
                            for it in items:
                                kind, args = it[0], it[1:]
                                if kind == "norm":
                                    u = args[0]
                                    g, t, h = unit(u)
                                    lo, hi = keys_of(t)
                                    p = probs[:, u % RING, lo:hi]
                                    wait_alone(pool, inverted, done(b, UNITS // 2, u // 2))
                                    pool.tensor_scalar(p, p, row_inv[:, u % RING:u % RING + 1], 1.0,
                                                       ALU.mult, ALU.mult).then_inc(normed, 1)
                                elif kind == "res_bias":
                                    t = args[0]
                                    wait_alone(pool, got_res[t % 2], b * (8 * NT) + (16 * (t // 2 + 1) - 8 * NT))
                                    pool.tensor_tensor(res[:, t % 2, :], res[:, t % 2, :], bias_o[:],
                                                       ALU.add).then_inc(res_ready, 1)

                        pool.wait_ge(got_const, 80)
                        rounds2(pool, walk)

                    @block.scalar
                    def _(act):
                        def walk(items, b):
                            for it in items:
                                kind, args = it[0], it[1:]
                                if kind == "exp":
                                    u = args[0]
                                    g, t, h = unit(u)
                                    lo, hi = keys_of(t)
                                    act.wait_ge(transposed, done(b, UNITS, u - RING))
                                    act.wait_ge(masked, done(b, UNITS, u))
                                    act.activation(probs[:, u % RING, lo:hi], neg_scores[:, u % NSM, lo:hi], ACT.Exp,
                                                   bias=neg_max[:, u % RING:u % RING + 1], scale=-1.0,
                                                   accum_out=row_sum[:, u % RING:u % RING + 1]).then_inc(exped, 1)
                                elif kind == "turn" and args[0] % 2 == 0:
                                    move_turned(act, args[0], b)
                                elif kind == "o_hi":
                                    g, half = args
                                    if g not in range(HELD):
                                        act.wait_ge(out_full, done(b, NT, (half - 1) * (NT // 2) - 1 - (
                                            0 if g > 0 else NT)))
                                    elif not (isinstance(b, int) and b == 0):
                                        act.wait_ge(o_moved, b * 32)
                                    act.wait_ge(pv_done, done(b, PV_TOTAL, pv_number(g, NT // 2 if half == 0 else NT - 1, half)))
                                    act.copy(o_place(0, g, half), o_bank[:]).then_inc(o_hi, 1)

                        rounds2(act, walk)

                    @block.vector
                    def _(dve):
                        def walk(items, b):
                            for it in items:
                                kind, args = it[0], it[1:]
                                if kind == "score":
                                    u = args[0]
                                    g, t, h = unit(u)
                                    lo, hi = keys_of(t)
                                    wait_alone(dve, exped, done(b, UNITS, u - NSM))
                                    wait_alone(dve, scores, done(b, UNITS, u))
                                    dve.tensor_tensor_reduce(out=neg_scores[:, u % NSM, lo:hi],
                                                             in0=score_bank[ring_slot(u)][:, lo:hi], in1=window[:, lo:hi],
                                                             scale=-SCALE, scalar=BIG, op0=ALU.add, op1=ALU.min,
                                                             accum_out=neg_max[:, u % RING:u % RING + 1]
                                                             ).then_inc(masked, 1)
                                elif kind == "invert":
                                    u = 2 * args[0]
                                    wait_alone(dve, normed, done(b, UNITS, u + 1 - RING))
                                    wait_alone(dve, exped, done(b, UNITS, u + 1))
                                    dve.reciprocal(row_inv[:, u % RING:u % RING + 2],
                                                   row_sum[:, u % RING:u % RING + 2]).then_inc(inverted, 1)
                                elif kind == "turn" and args[0] % 2 == 1:
                                    move_turned(dve, args[0], b)
                                elif kind == "o_lo":
                                    g, half = args
                                    wait_alone(dve, o_hi, done(b, 2 * C, 2 * g + half))
                                    dve.tensor_tensor(o_place(1, g, half), o_bank[:],
                                                      o_place(0, g, half).bitcast(F32),
                                                      ALU.subtract).then_inc(o_free, 1)
                                elif kind == "out_evac":
                                    t = args[0]
                                    wait_alone(dve, res_ready, done(b, NT, t - NT))
                                    wait_alone(dve, out_full, done(b, NT, t - NT))
                                    dve.tensor_tensor(res[:, t % 2, :], out_place(t, b)[:], res[:, t % 2, :],
                                                      ALU.add).then_inc(out_free, 1)

                        rounds2(dve, walk)

                    @block.tensor
                    def _(pe):
                        def walk(items, b):
                            for it in items:
                                kind, args = it[0], it[1:]
                                if kind == "score":
                                    u = args[0]
                                    g, t, h = unit(u)
                                    lo, hi = keys_of(t)
                                    if u % GROUP == 0:
                                        pe.wait_ge(got_qk[g % 2], b * (LOAD_QK * C // 2) + LOAD_QK * (g // 2 + 1))
                                    pe.wait_ge(masked, done(b, UNITS, earlier_in_ring(u)))
                                    pe.matmul(score_bank[ring_slot(u)][:, lo:hi],
                                              stack["q"][g % 2][0:3 * DK, h, t * P:t * P + P],
                                              stack["k"][g % 2][0:3 * DK, h, (t - 1) * P + lo:(t - 1) * P + hi],
                                              start=True, stop=True).then_inc(scores, 1)
                                elif kind == "turn":
                                    u = args[0]
                                    g, t, h = unit(u)
                                    lo, hi = keys_of(t)
                                    earlier = earlier_in_ring(u)
                                    moved = pt_by_act if earlier % 2 == 0 else pt_by_dve
                                    pe.wait_ge(moved, done(b, UNITS // 2, earlier // 2))
                                    pe.wait_ge(normed, done(b, UNITS, u))
                                    for col in range(lo, hi, P):
                                        last = pe.transpose(turn_bank[ring_slot(u)][:, col:col + P],
                                                            probs[:, u % RING, col:col + P], ident[:])
                                    last.then_inc(transposed, 1)
                                elif kind == "pv":
                                    g, k, half = args
                                    q0 = max(k - 1, half * NT // 2)
                                    q1 = min(k + 2, (half + 1) * NT // 2)
                                    for moved in (pt_by_act, pt_by_dve):
                                        pe.wait_ge(moved, done(b, UNITS // 2, (g * NT + q1) * HG // 2 - 1))
                                    begins = (k, half) in ((0, 0), (NT // 2 - 1, 1))
                                    if begins:
                                        pe.wait_ge(o_free, done(b, 2 * C, 2 * g + half - 1))
                                    if k == 0:
                                        pe.wait_ge(got_v[g % 2], b * (16 * C // 2) + 16 * (g // 2 + 1))
                                    for h in range(HG):
                                        pieces = probs_t[:, q0 % NQT:q0 % NQT + q1 - q0, h, :]
                                        first_col = (k - q0 + 1) * P
                                        moving = diagonal(pieces, first_col, q1 - q0)
                                        col = (q0 * P) % HALF
                                        out_cols = o_bank[DK * h:DK * h + DK, col:col + (q1 - q0) * P]
                                        last = pe.matmul(out_cols.rearrange("p (q n) -> p q n", n=P),
                                                         v_group[g % 2][:, k, h * DK:(h + 1) * DK], moving,
                                                         start=begins, stop=True, skip_group_check=True)
                                    last.then_inc(pv_done, 1)
                                elif kind == "out":
                                    t, piece = args
                                    bank = out_place(t, b)
                                    if piece == 0:
                                        pe.wait_ge(o_moved, b * 32)
                                        pe.wait_ge(o_free, done(b, 2 * C, t // (NT // 2) - 2))
                                        pe.wait_ge(out_free, done(b, NT, t - NT - (2 if isinstance(b, int) and b == B else 1)))
                                    products = [(c, a, v) for c in range(C) for a, v in PRODUCTS]
                                    per_piece = 3 * C // len(OUT_PIECES)
                                    for m in range(piece * per_piece, (piece + 1) * per_piece):
                                        c, a, v = products[m]
                                        last = pe.matmul(bank[:], o_t[a][:, c, t * P:t * P + P], wo_w[v][:, c, :],
                                                         start=(m == 0), stop=(m == 3 * C - 1))
                                    if piece == len(OUT_PIECES) - 1:
                                        last.then_inc(out_full, 1)

                        def diagonal(pieces, first_col, count):
                            ap = pieces[:, :, first_col:first_col + P]
                            if count == 1:
                                return ap
                            steps_ = [list(d) for d in ap.ap]
                            steps_[1][0] -= P
                            return bass.AP(tensor=ap.tensor, offset=ap.offset, ap=steps_)

                        rounds2(pe, walk)

        with ExitStack() as phase3:
            def sb(name, shape, dt=F32):
                return phase3.enter_context(nc.sbuf_tensor(name, shape, dt))

            keys_w = [sb(f"keys_{n}", [P, NE, C, P], F32R) for n in ("hi", "lo")]
            values_w = [sb(f"values_{n}", [P, NE, D], F32R) for n in ("hi", "lo")]
            sel_w = [sb(f"sel_{n}", [P, C, P], F32R) for n in ("hi", "lo")]

            x2 = [sb(f"x2_{par}", [P, TB, D]) for par in range(2)]
            x2_norm = sb("x2_norm", [P, 2, D])
            st2, mv2, rs2 = sb("st2", [P, 2, 6]), sb("mv2", [P, 2, 2]), sb("rs2", [P, 2, 1])
            x2_t = [[sb(f"x2_t{par}_{n}", [P, C, BLK], F32R) for n in ("hi", "lo")] for par in range(2)]
            gated_f = sb("gated_f", [P, 2, BLK])
            gated_w = [sb(f"gated_{n}", [P, 2, BLK], F32R) for n in ("hi", "lo")]
            gate_sb = sb("gate_sb", [P, NGATE, BLK])
            logits_sb, gates_t = x2_norm[0:NE, 0, :], x2_norm[0:NE, 1, :]
            exps = sb("exps", [P, TB, NE])
            router = sb("router", [P, TB, NE + TOPK])
            rest = sb("rest", [P, TB, NE + TOPK])
            top8, taken = sb("top8", [P, TB, 8]), sb("taken", [P, TB, 8])
            row = sb("row", [P, 4, TB])
            gates = sb("gates", [P, 2, TB, NE])
            out_bank, hidden_bank, misc_bank = psum[0:4], psum[4:6], psum[6:8]
            w_stage = [buffer.rearrange("p t d -> p (t d)")
                       for buffer in (x2[1][:, 0:2], x2[1][:, 2:4], gated_f[:], gate_sb[:, 2:4])]
            ROUTE_OWN = 8 + TB * 2

            def split_place(what, e, part):
                if what == "keys":
                    return keys_w[part][:, e:e + PER_LOAD].rearrange("p e c h -> p (e c h)")
                return values_w[part][:, e:e + PER_LOAD].rearrange("p e n -> p (e n)")

            def split_number(steps, it):
                return steps.ordinal[it] - 1

            def gate_value(b, par, e, is_first):
                blocks = 0 if is_first else 2 if (par, e) == (0, 0) else par
                return b * (32 * NE // NGATE) + (blocks * (16 * NE // NGATE) + 16 * (e // NGATE + 1))

            first3 = first_block_steps()
            steady3 = Steps(block_steps(0, False) + block_steps(1, False))
            final3 = Steps(block_steps(0, False) + block_steps(1, True))
            rounds3 = rounds_of(first3, steady3, final3, NB // 2 - 1)

            with nc.Block() as block:
                @block.sync
                def _(sp):
                    def walk(steps, n, b, is_first):
                        base = b * (2 * BLK) if isinstance(b, int) else sp.snap(b * (2 * BLK))
                        for it in steps.items:
                            kind, args = it[0], it[1:]
                            if kind == "load_x2":
                                par = args[0]
                                at = base if is_first else base + (BLK if par else 2 * BLK)
                                wait_alone(sp, out_stored[par], b * (16 * TB) + (CREDIT + (0 if is_first or par else 16 * TB)))
                                sp.dma_start(x2[par][:], x2f[bass.ds(at, BLK), :].rearrange("(t p) d -> p t d", p=P)
                                             ).then_inc(got_x2[par], 16)
                            elif kind == "split":
                                what, e = args
                                number = split_number(steps, it)
                                if number >= NWSTAGE:
                                    sp.wait_ge(split_lo, number - NWSTAGE + 1)
                                dst = w_stage[number % NWSTAGE]
                                if what == "keys":
                                    src = keys[e:e + PER_LOAD].rearrange("e (c p) h -> p (e c) h", p=P)
                                    dst = dst.rearrange("p (ec h) -> p ec h", h=P)
                                else:
                                    src = values[e:e + PER_LOAD].rearrange("e h n -> h e n")
                                    dst = dst.rearrange("p (e n) -> p e n", n=D)
                                sp.dma_start(dst, src).then_inc(got_stage[number % NWSTAGE], 16)
                            elif kind == "gate_store":
                                par = args[0]
                                wait_alone(sp, gates_out, n.upto(("gates_evac", par)))
                                sp.dma_start(gate_scratch[par], gates_t[:]).then_inc(gate_stored[par], 16)
                            elif kind == "gate":
                                par, e = args
                                if is_first and e == 2:
                                    sp.wait_ge(split_lo, 2 * NE // PER_LOAD)
                                if e == 0:
                                    wait_alone(sp, gate_stored[par], b * 16 + (16 if is_first or par else 32))
                                wait_alone(sp, gated, n.upto(it, NGATE))
                                sp.dma_start(gate_sb[:, e % NGATE, :], gate_scratch[par][e].partition_broadcast(P)
                                             ).then_inc(got_gate[e % NGATE], 16)
                            elif kind == "final":
                                par, t = args
                                wait_alone(sp, finals, n.upto(it))
                                sp.dma_start(outf[bass.ds(base + (par * BLK + t * P), P), :],
                                             x2[par][:, t, :]).then_inc(out_stored[par], 16)

                    rounds3(sp, walk)
                    for s in out_stored:
                        sp.wait_ge(s, CREDIT + 16 * TB * (NB // 2))

                @block.gpsimd
                def _(pool):
                    def walk(steps, n, b, is_first):
                        for it in steps.items:
                            if it[0] == "ln3_rstd":
                                _, par, t = it
                                wait_alone(pool, stats3, n.upto(("ln3_stats", par, t)))
                                pool.tensor_tensor(rs2[:, t % 2, :], mv2[:, t % 2, 1:2], half_neg[:],
                                                   ALU.pow).then_inc(rstd3, 1)

                    rounds3(pool, walk)

                @block.scalar
                def _(act):
                    def walk(steps, n, b, is_first):
                        for it in steps.items:
                            kind, args = it[0], it[1:]
                            if kind == "split":
                                number = split_number(steps, it)
                                act.wait_ge(got_stage[number % NWSTAGE], 16 * (number // NWSTAGE + 1))
                                act.copy(split_place(*args, 0), w_stage[number % NWSTAGE]).then_inc(split_hi, 1)
                            elif kind == "hidden":
                                par, e = args
                                act.wait_ge(value_done, n.ahead("value", it))
                                act.wait_ge(gated, n.upto(it))
                                act.copy(gated_w[0][:, e % 2, :], gated_f[:, e % 2, :]).then_inc(gated_hi, 1)
                            elif kind == "turn2_evac":
                                par, t = args
                                act.wait_ge(turned2, n.upto(("turn2", par, t)))
                                act.copy(x2_t[par][0][:, :, t * P:t * P + P],
                                         misc_bank[t % 2][:].rearrange("p (c n) -> p c n", c=C)
                                         ).then_inc(x2t_hi, 1)
                            elif kind == "sigmoid":
                                act.wait_ge(logits_tok, n.upto(("logits_turn", args[0])))
                                act.activation(exps[:].rearrange("p t e -> p (t e)"), misc_bank[1][:, 0:TB * NE],
                                               ACT.Exp, scale=-1.0).then_inc(router_exp, 1)

                    rounds3(act, walk)

                @block.vector
                def _(dve):
                    for m in (router, taken):
                        dve.memset(m[:], -1.0)
                    for part in range(2):
                        dve.memset(sel_w[part][:].bitcast(F32), 0.0).then_inc(sel_split, 1)
                    dve.wait_ge(sel_split, 2)
                    dve.tensor_copy(sel_w[0][:, :, 0:NE], sel_t[:]).then_inc(sel_split, 1)
                    dve.wait_ge(sel_split, 3)
                    dve.tensor_tensor(sel_w[1][:, :, 0:NE], sel_t[:], sel_w[0][:, :, 0:NE].bitcast(F32),
                                      ALU.subtract).then_inc(sel_split, 1)
                    dve.drain()

                    def walk(steps, n, b, is_first):
                        per_block = 2 * TB + ROUTE_OWN
                        before = 0 if is_first else per_block
                        k = 0

                        def link(*instructions):
                            nonlocal k
                            k += len(instructions)
                            for instruction in instructions:
                                instruction.then_inc(dve_linked, 1)
                            wait_alone(dve, dve_linked, b * (2 * per_block) + (before + k))

                        for it in steps.items:
                            kind, args = it[0], it[1:]
                            if kind == "split":
                                number = split_number(steps, it)
                                dve.wait_ge(split_hi, number + 1)
                                dve.tensor_tensor(split_place(*args, 1), w_stage[number % NWSTAGE],
                                                  split_place(*args, 0).bitcast(F32),
                                                  ALU.subtract).then_inc(split_lo, 1)
                            elif kind == "ln3_stats":
                                par, t = args
                                if t == 0:
                                    if not is_first:
                                        wait_alone(dve, gate_stored[1 - par], b * 16 + 16)
                                    wait_alone(dve, got_x2[par], b * 16 + (16 if is_first or par else 32))
                                link(dve.bn_stats(st2[:, t % 2, :], x2[par][:, t, :]))
                                link(dve.bn_aggr(mv2[:, t % 2, :], st2[:, t % 2, :]))
                                dve.tensor_scalar(mv2[:, t % 2, 1:2], mv2[:, t % 2, 1:2], EPS, None,
                                                  ALU.add).then_inc(stats3, 1)
                            elif kind == "ln3_apply":
                                par, t = args
                                wait_alone(dve, rstd3, n.upto(("ln3_rstd", par, t)))
                                dve.tensor_scalar(x2_norm[:, t % 2, :], x2[par][:, t, :], mv2[:, t % 2, 0:1],
                                                  rs2[:, t % 2, :], ALU.subtract, ALU.mult).then_inc(xn3, 1)
                            elif kind == "turn2_evac":
                                par, t = args
                                wait_alone(dve, x2t_hi, n.upto(it))
                                dve.tensor_tensor(x2_t[par][1][:, :, t * P:t * P + P],
                                                  misc_bank[t % 2][:].rearrange("p (c n) -> p c n", c=C),
                                                  x2_t[par][0][:, :, t * P:t * P + P].bitcast(F32),
                                                  ALU.subtract).then_inc(x2t_ready, 1)
                            elif kind == "logits_evac":
                                wait_alone(dve, logits_done, n.upto(("logits", args[0])))
                                dve.tensor_copy(logits_sb[:], misc_bank[0][0:NE, :]).then_inc(logits_out, 1)
                            elif kind == "sigmoid":
                                wait_alone(dve, router_exp, n.upto(it))
                                link(dve.tensor_scalar(exps[:], exps[:], 1.0, None, ALU.add))
                                link(dve.reciprocal(router[:, :, 0:NE], exps[:]))
                                link(*[dve.max(top8[:, t, :], router[:, t, 0:NE]) for t in range(TB)])
                            elif kind == "choose":
                                link(dve.tensor_copy(taken[:, :, 0:TOPK], top8[:, :, 0:TOPK]),
                                     dve.reduce_sum(row[:, 0, :], top8[:, :, 0:TOPK], axis=AX_X))
                                replaced = [dve.match_replace(out=rest[:, t, :], in_to_replace=taken[:, t, :],
                                                              in_values=router[:, t, :], imm_value=0.0)
                                            for t in range(TB)]
                                link(*replaced, dve.tensor_scalar(row[:, 1, :], row[:, 0, :], 1e-9, None, ALU.max))
                                link(dve.reciprocal(row[:, 2, :], row[:, 1, :]))
                                link(dve.tensor_scalar(row[:, 3, :], row[:, 2, :], scale_col[:], None, ALU.mult),
                                     dve.tensor_tensor(gates[:, 0], router[:, :, 0:NE], rest[:, :, 0:NE],
                                                       ALU.subtract))
                            elif kind == "weigh":
                                for t in range(TB):
                                    last = dve.tensor_scalar(gates[:, 1, t, :], gates[:, 0, t, :], row[:, 3, t:t + 1],
                                                             None, ALU.mult)
                                last.then_inc(gates_ready, 1)
                            elif kind == "gates_evac":
                                par = args[0]
                                wait_alone(dve, gates_turned, n.upto(("gates_turn", par)))
                                dve.tensor_copy(gates_t[:], misc_bank[1][0:NE, :]).then_inc(gates_out, 1)
                            elif kind == "hidden":
                                par, e = args
                                if is_first:
                                    dve.wait_ge(split_lo, 2 * NE // PER_LOAD)
                                wait_alone(dve, gated_hi, n.upto(it, 2))
                                wait_alone(dve, gated_lo, n.upto(it, 2))
                                wait_alone(dve, got_gate[e % NGATE], gate_value(b, par, e, is_first))
                                wait_alone(dve, hidden_full, n.upto(it))
                                dve.scalar_tensor_tensor(out=gated_f[:, e % 2, :], in0=hidden_bank[e % 2][:],
                                                         scalar=0.0, in1=gate_sb[:, e % NGATE, :], op0=ALU.max,
                                                         op1=ALU.mult).then_inc(gated, 1)
                                wait_alone(dve, value_done, n.ahead("value", it))
                                wait_alone(dve, gated_hi, n.upto(it))
                                dve.tensor_tensor(gated_w[1][:, e % 2, :], gated_f[:, e % 2, :],
                                                  gated_w[0][:, e % 2, :].bitcast(F32),
                                                  ALU.subtract).then_inc(gated_lo, 1)
                            elif kind == "final":
                                par, t = args
                                wait_alone(dve, value_done, n.upto(("value", par, NE - 1)))
                                dve.tensor_tensor(x2[par][:, t, :], out_bank[t][:], x2[par][:, t, :],
                                                  ALU.add).then_inc(finals, 1)

                    rounds3(dve, walk)

                @block.tensor
                def _(pe):
                    def walk(steps, n, b, is_first):
                        for it in steps.items:
                            kind, args = it[0], it[1:]
                            if kind == "settle":
                                pe.wait_ge(split_lo, 2 * NE // PER_LOAD)
                            elif kind == "hidden":
                                par, e = args
                                pe.wait_ge(gated, n.upto(it, 2))
                                if is_first:
                                    pe.wait_ge(split_lo, 1)
                                if e == 0:
                                    pe.wait_ge(x2t_ready, n.upto(("turn2_evac", par, TB - 1)))
                                for m, (c, a, m_x) in enumerate([(c, a, m_x) for c in range(C) for a, m_x in PRODUCTS]):
                                    last = pe.matmul(hidden_bank[e % 2][:], keys_w[a][:, e, c, :],
                                                     x2_t[par][m_x][:, c, :], start=(m == 0), stop=(m == 3 * C - 1))
                                last.then_inc(hidden_full, 1)
                            elif kind == "value":
                                par, e = args
                                pe.wait_ge(gated_hi, n.ahead("value", it) + 1)
                                pe.wait_ge(gated_lo, n.ahead("value", it) + 1)
                                for t in range(TB):
                                    if e == 0:
                                        pe.wait_ge(finals, n.ahead("final", it, TB - 1 - t))
                                    for m, (a, v) in enumerate(PRODUCTS):
                                        last = pe.matmul(out_bank[t][:], gated_w[a][:, e % 2, t * P:t * P + P],
                                                         values_w[v][:, e, :], start=(e == 0 and m == 0),
                                                         stop=(e == NE - 1 and m == 2))
                                last.then_inc(value_done, 1)
                            elif kind == "turn2":
                                par, t = args
                                pe.wait_ge(x2t_ready, n.ahead("turn2_evac", it, 1))
                                pe.wait_ge(gates_out, n.ahead("gates_evac", it))
                                pe.wait_ge(xn3, n.upto(("ln3_apply", par, t)))
                                for c in range(C):
                                    last = pe.transpose(misc_bank[t % 2][:, c * P:c * P + P],
                                                        x2_norm[:, t % 2, c * P:c * P + P], ident[:])
                                last.then_inc(turned2, 1)
                            elif kind == "logits":
                                par = args[0]
                                if is_first:
                                    pe.wait_ge(sel_split, 4)
                                pe.wait_ge(x2t_ready, n.ahead("turn2_evac", it))
                                for m, (c, a, m_x) in enumerate([(c, a, m_x) for c in range(C) for a, m_x in PRODUCTS]):
                                    last = pe.matmul(misc_bank[0][:], sel_w[a][:, c, :], x2_t[par][m_x][:, c, :],
                                                     start=(m == 0), stop=(m == 3 * C - 1))
                                last.then_inc(logits_done, 1)
                            elif kind == "logits_turn":
                                wait_alone(pe, logits_out, n.upto(("logits_evac", args[0])))
                                for t in range(TB):
                                    last = pe.transpose(misc_bank[1][:, t * NE:t * NE + NE],
                                                        logits_sb[:, t * P:t * P + P], ident[0:NE, 0:NE])
                                last.then_inc(logits_tok, 1)
                            elif kind == "gates_turn":
                                wait_alone(pe, gates_ready, n.upto(("weigh", args[0])))
                                for t in range(TB):
                                    last = pe.transpose(misc_bank[1][0:NE, t * P:t * P + P], gates[:, 1, t, :],
                                                        ident[:])
                                last.then_inc(gates_turned, 1)

                    rounds3(pe, walk)


INPUTS = ["x", "ctx_1024", "L0_xattn_Wq", "L0_xattn_bq", "L0_xattn_Wk", "L0_xattn_bk", "L0_xattn_Wv", "L0_xattn_bv",
          "L0_xattn_Wo", "L0_xattn_bo", "L0_ffn_expert_sel", "L0_ffn_keys", "L0_ffn_values", "L0_ffn_route_scale"]


def kernel(**inputs):
    import numpy as np
    import concourse.bacc as bacc
    from concourse.bass_utils import run_bass_kernel_spmd

    nc = bacc.Bacc("TRN2", target_bir_lowering=False, num_devices=1)
    arrays, args = {}, []
    for name in INPUTS:
        a = np.ascontiguousarray(inputs[name])
        arrays[name + "_dram"] = a
        args.append(nc.dram_tensor(name + "_dram", a.shape, mybir.dt.from_np(a.dtype), kind="ExternalInput").ap())
    args.append(nc.dram_tensor("out_dram", (B, SEQ, D), F32, kind="ExternalOutput").ap())
    build_kernel(nc, *args)
    result = run_bass_kernel_spmd(nc, [arrays], core_ids=[0])
    return result.results[0]["out_dram"]
```
